# Optimizing a Trainium2 kernel written in Bass

```python
import numpy as np
import jax
import jax.numpy as jnp

def _softmax(x, axis=-1):
    return jax.nn.softmax(x, axis=axis)

def _gelu(x):
    return jax.nn.gelu(x, approximate=True)

def _silu(x):
    return jax.nn.silu(x)

def _sigmoid(x):
    return jax.nn.sigmoid(x)

def _layernorm(x, axis=-1, eps=1e-05):
    m = jnp.mean(x, axis=axis, keepdims=True)
    v = jnp.var(x, axis=axis, keepdims=True)
    return (x - m) / jnp.sqrt(v + eps)

def _scatter_add(tgt, idx, src, axis=0):
    return tgt.at[idx].add(src)

def _segment_sum(src, seg, n):
    return jax.ops.segment_sum(src, seg, n)
kernel_name = 'mk_gnn_ffn_d4_gnn_r16_d9afd5'

def setup_inputs(seed: int=0):
    np.random.seed(seed)
    _w = jnp.asarray

    def _rec_inputs():
        import jax
        import jax.numpy as jnp
        _gk = jax.random.key(seed)
        x = -6.415e-05 + 1 * jax.random.normal(jax.random.fold_in(_gk, 1), (625, 512), jnp.float32)
        src = jax.random.randint(jax.random.fold_in(_gk, 2), (20000,), 0, 625, jnp.int32)
        dst = jnp.minimum((625 * jax.random.uniform(jax.random.fold_in(_gk, 3), (20000,)) ** 2.0).astype(jnp.int32), 9999)
        _o = jnp.argsort(dst, stable=True)
        src = src[_o]
        dst = dst[_o]
        edge_type_32 = jax.random.randint(jax.random.fold_in(_gk, 13), (20000,), 0, 32, jnp.int32)
        edge_weight = jax.random.uniform(jax.random.fold_in(_gk, 14), (20000,), jnp.float32, 0.0, 1)
        edge_weight1 = jax.random.uniform(jax.random.fold_in(_gk, 15), (20000, 1), jnp.float32, 0.0, 0.999996)
        return (x, src, dst, edge_type_32, edge_weight, edge_weight1)
    x, src, dst, edge_type_32, edge_weight, edge_weight1 = _rec_inputs()

    def _L0_gnn_setup():
        import jax, jax.numpy as jnp
        import numpy as np
        N_NODES = 1250
        N_EDGES = 9375
        IN_C = 512
        OUT_C = 512
        K_INIT = 7

        def _spmm(row, col, lap, x, num_nodes):
            msgs = lap[:, None] * x[col]
            return jax.ops.segment_sum(msgs, row, num_segments=num_nodes)
        key = jax.random.key(seed)
        k1, k2, k3, k4 = jax.random.split(key, 4)
        x = jax.random.normal(k1, (N_NODES, IN_C), dtype=jnp.float32)
        edge_index = jax.random.randint(k2, (2, N_EDGES), 0, N_NODES, dtype=jnp.int32)
        bound = 1.0 / np.sqrt(IN_C * (K_INIT + 1))
        weight = jax.random.uniform(k3, (K_INIT + 1, IN_C, OUT_C), dtype=jnp.float32, minval=-bound, maxval=bound)
        bias = jax.random.uniform(k4, (OUT_C,), dtype=jnp.float32, minval=-bound, maxval=bound)
        return {'x': x, 'edge_index': edge_index, 'weight': weight, 'bias': bias}
    _L0_gnn_all = _L0_gnn_setup()
    _L0_gnn_in = {k: v for k, v in _L0_gnn_all.items() if k in ('weight', 'bias')}
    del _L0_gnn_all

    def _L0_ffn_setup():
        import jax, jax.numpy as jnp
        import numpy as np
        B, S, D, E, O = (1024, 256, 512, 16, 512)
        key = jax.random.key(seed)
        k_x, k_wg, k_bg, k_we, k_be = jax.random.split(key, 5)
        scale_g = 1.0 / np.sqrt(D)
        scale_e = 1.0 / np.sqrt(D)
        return {'x': jax.random.normal(k_x, (B, S, D), dtype=jnp.float32), 'Wg': jax.random.uniform(k_wg, (D, E), jnp.float32, -scale_g, scale_g), 'bg': jax.random.uniform(k_bg, (E,), jnp.float32, -scale_g, scale_g), 'We': jax.random.uniform(k_we, (E, D, O), jnp.float32, -scale_e, scale_e), 'be': jax.random.uniform(k_be, (E, O), jnp.float32, -scale_e, scale_e)}
    _L0_ffn_all = _L0_ffn_setup()
    _L0_ffn_in = {k: v for k, v in _L0_ffn_all.items() if k in ('Wg', 'bg', 'We', 'be')}
    del _L0_ffn_all

    def _L1_gnn_setup():
        import jax, jax.numpy as jnp
        import numpy as np
        N = 3125
        E = 100000
        F_IN = 512
        H = 128
        key = jax.random.key(seed)
        k0, k1, k2, k3 = jax.random.split(key, 4)
        x = jax.random.normal(k0, (N, F_IN), dtype=jnp.float32)
        edge_index = jax.random.randint(k1, (2, E), 0, N, dtype=jnp.int32)
        edge_weight = jnp.ones((E,), dtype=jnp.float32)
        W_conv = jax.random.normal(k2, (F_IN, H), dtype=jnp.float32) * np.sqrt(2.0 / (F_IN + H)).astype(np.float32)
        b_conv = jnp.zeros((H,), dtype=jnp.float32)
        W_lin = jax.random.normal(k3, (H, F_IN), dtype=jnp.float32) * np.sqrt(2.0 / (H + F_IN)).astype(np.float32)
        b_lin = jnp.zeros((F_IN,), dtype=jnp.float32)
        return {'x': x, 'edge_index': edge_index, 'edge_weight': edge_weight, 'W_conv': W_conv, 'b_conv': b_conv, 'W_lin': W_lin, 'b_lin': b_lin}
    _L1_gnn_all = _L1_gnn_setup()
    _L1_gnn_in = {k: v for k, v in _L1_gnn_all.items() if k in ('W_conv', 'b_conv', 'W_lin', 'b_lin')}
    del _L1_gnn_all

    def _L1_ffn_setup():
        import jax, jax.numpy as jnp
        import numpy as np
        EPS = 1e-06
        SINKHORN_ITERS = 8
        TEMPERATURE = 1.0
        B, N, D = (4, 512, 512)
        E, OUT = (8, 512)
        H = 1

        def _sinkhorn(logits):
            t = jnp.log(jnp.clip(logits, EPS)) / TEMPERATURE
            for _ in range(SINKHORN_ITERS):
                t = t - jax.nn.logsumexp(t, axis=-2, keepdims=True)
                t = t - jax.nn.logsumexp(t, axis=-1, keepdims=True)
            return jnp.exp(t)
        key = jax.random.key(seed)
        k1, k2, k3 = jax.random.split(key, 3)
        x = jax.random.normal(k1, (B, N, D), dtype=jnp.float32)
        gate_weight = jax.random.normal(k2, (H, D, E), dtype=jnp.float32)
        experts = jax.random.normal(k3, (E, D, OUT), dtype=jnp.float32) * 0.02
        return {'x': x, 'gate_weight': gate_weight, 'experts': experts}
    _L1_ffn_all = _L1_ffn_setup()
    _L1_ffn_in = {k: v for k, v in _L1_ffn_all.items() if k in ('gate_weight', 'experts')}
    del _L1_ffn_all

    def _L2_gnn_setup():
        import jax, jax.numpy as jnp
        import numpy as np
        N_NODES = 1250
        N_EDGES = 20000
        IN_FEAT = 512
        OUT_FEAT = 512
        NUM_RELS = 32
        NUM_BASES = 8
        key = jax.random.key(seed)
        ks = jax.random.split(key, 8)
        x = jax.random.normal(ks[0], (N_NODES, IN_FEAT), dtype=jnp.float32)
        bases = jax.random.normal(ks[1], (NUM_BASES, IN_FEAT, OUT_FEAT), dtype=jnp.float32) * (1.0 / np.sqrt(IN_FEAT))
        w_comp = jax.random.normal(ks[2], (NUM_RELS, NUM_BASES), dtype=jnp.float32) * (1.0 / np.sqrt(NUM_BASES))
        h_bias = jnp.zeros((OUT_FEAT,), dtype=jnp.float32)
        norm = jax.random.uniform(ks[3], (N_EDGES, 1), dtype=jnp.float32)
        src = jax.random.randint(ks[4], (N_EDGES,), 0, N_NODES, dtype=jnp.int32)
        dst = jax.random.randint(ks[5], (N_EDGES,), 0, N_NODES, dtype=jnp.int32)
        etype = jnp.sort(jax.random.randint(ks[6], (N_EDGES,), 0, NUM_RELS, dtype=jnp.int32))
        return {'x': x, 'bases': bases, 'w_comp': w_comp, 'h_bias': h_bias, 'norm': norm, 'src': src, 'dst': dst, 'etype': etype}
    _L2_gnn_all = _L2_gnn_setup()
    _L2_gnn_in = {k: v for k, v in _L2_gnn_all.items() if k in ('bases', 'w_comp', 'h_bias')}
    del _L2_gnn_all

    def _L2_ffn_setup():
        import jax, jax.numpy as jnp
        import numpy as np
        B, T, I, H, S = (64, 128, 512, 512, 4)

        def _lstm_activate(gates, c):
            i, f, g, o = jnp.split(gates, 4, axis=-1)
            c_new = jax.nn.sigmoid(f) * c + jax.nn.sigmoid(i) * jnp.tanh(g)
            h_new = jax.nn.sigmoid(o) * jnp.tanh(c_new)
            return (h_new, c_new)
        key = jax.random.key(seed)
        ks = jax.random.split(key, 7)
        sc_i = 1.0 / np.sqrt(I)
        sc_h = 1.0 / np.sqrt(H)
        x = jax.random.normal(ks[0], (B, T, I), jnp.float32)
        W_ih = jax.random.normal(ks[1], (S, 4 * H, I), jnp.float32) * sc_i
        W_hh = jax.random.normal(ks[2], (S, 4 * H, H), jnp.float32) * sc_h
        b_ih = jax.random.normal(ks[3], (S, 4 * H), jnp.float32) * sc_h
        b_hh = jax.random.normal(ks[4], (S, 4 * H), jnp.float32) * sc_h
        W_sel = jax.random.normal(ks[5], (S, 2 * H + I), jnp.float32) * sc_h
        b_sel = jax.random.normal(ks[6], (S,), jnp.float32) * sc_h
        return {'x': x, 'W_ih': W_ih, 'W_hh': W_hh, 'b_ih': b_ih, 'b_hh': b_hh, 'W_sel': W_sel, 'b_sel': b_sel}
    _L2_ffn_all = _L2_ffn_setup()
    _L2_ffn_in = {k: v for k, v in _L2_ffn_all.items() if k in ('W_ih', 'W_hh', 'b_ih', 'b_hh', 'W_sel', 'b_sel')}
    del _L2_ffn_all

    def _L3_gnn_setup():
        import jax, jax.numpy as jnp
        import numpy as np
        N_NODES = 625
        N_EDGES = 10000
        IN_DIM = 512
        HID = 256
        HEADS = 4
        OUT_DIM = 512
        NEG_SLOPE = 0.2

        def _glorot(key, shape):
            fan_in, fan_out = (shape[0], shape[-1])
            lim = jnp.sqrt(6.0 / (fan_in + fan_out))
            return jax.random.uniform(key, shape, jnp.float32, -lim, lim)

        def gat_conv(x, src, dst, W, att_src, att_dst, bias):
            N = x.shape[0]
            h = (x @ W).reshape(N, HEADS, HID)
            a_src = jnp.sum(h * att_src, axis=-1)
            a_dst = jnp.sum(h * att_dst, axis=-1)
            e = jax.nn.leaky_relu(a_src[src] + a_dst[dst], NEG_SLOPE)
            m = jax.ops.segment_max(e, dst, num_segments=N)
            e = jnp.exp(e - m[dst])
            s = jax.ops.segment_sum(e, dst, num_segments=N)
            alpha = e / (s[dst] + 1e-16)
            msg = alpha[:, :, None] * h[src]
            out = jax.ops.segment_sum(msg, dst, num_segments=N)
            return out.reshape(N, HEADS * HID) + bias
        key = jax.random.key(seed)
        ks = jax.random.split(key, 16)
        x = jax.random.normal(ks[0], (N_NODES, IN_DIM), jnp.float32)
        edge_index = jax.random.randint(ks[1], (2, N_EDGES), 0, N_NODES, jnp.int64)
        W1 = _glorot(ks[2], (IN_DIM, HEADS * HID))
        att_src1 = _glorot(ks[3], (HEADS, HID))
        att_dst1 = _glorot(ks[4], (HEADS, HID))
        b1 = jnp.zeros((HEADS * HID,), jnp.float32)
        W2 = _glorot(ks[5], (HEADS * HID, HEADS * HID))
        att_src2 = _glorot(ks[6], (HEADS, HID))
        att_dst2 = _glorot(ks[7], (HEADS, HID))
        b2 = jnp.zeros((HEADS * HID,), jnp.float32)
        fcW = _glorot(ks[8], (HEADS * HID, OUT_DIM))
        fcb = jnp.zeros((OUT_DIM,), jnp.float32)
        return dict(x=x, edge_index=edge_index, W1=W1, att_src1=att_src1, att_dst1=att_dst1, b1=b1, W2=W2, att_src2=att_src2, att_dst2=att_dst2, b2=b2, fcW=fcW, fcb=fcb)
    _L3_gnn_all = _L3_gnn_setup()
    _L3_gnn_in = {k: v for k, v in _L3_gnn_all.items() if k in ('W1', 'att_src1', 'att_dst1', 'b1', 'W2', 'att_src2', 'att_dst2', 'b2', 'fcW', 'fcb')}
    del _L3_gnn_all

    def _L3_ffn_setup():
        import jax, jax.numpy as jnp
        import numpy as np
        D_MODEL = 512
        N_HEADS = 8
        KV_OPTS = (8, 4, 1)
        D_K = D_MODEL // N_HEADS

        def gqa(x, wq, wk, wv, wo, n_kv):
            B, S, _ = x.shape
            groups = N_HEADS // n_kv
            q = (x @ wq).reshape(B, S, N_HEADS, D_K).transpose(0, 2, 1, 3)
            k = (x @ wk).reshape(B, S, n_kv, D_K).transpose(0, 2, 1, 3)
            v = (x @ wv).reshape(B, S, n_kv, D_K).transpose(0, 2, 1, 3)
            k = jnp.repeat(k, groups, axis=1)
            v = jnp.repeat(v, groups, axis=1)
            scores = jnp.einsum('bhqd,bhkd->bhqk', q, k) / jnp.sqrt(jnp.float32(D_K))
            attn = jax.nn.softmax(scores, axis=-1)
            out = jnp.einsum('bhqk,bhkd->bhqd', attn, v)
            out = out.transpose(0, 2, 1, 3).reshape(B, S, D_MODEL)
            return out @ wo
        key = jax.random.key(seed)
        ks = jax.random.split(key, 32)
        it = iter(ks)
        s = 0.02
        inp = {'x': jax.random.normal(next(it), (64, 1024, D_MODEL), dtype=jnp.float32)}
        inp['r_w1'] = jax.random.normal(next(it), (D_MODEL, D_MODEL // 4), jnp.float32) * s
        inp['r_b1'] = jnp.zeros((D_MODEL // 4,), jnp.float32)
        inp['r_w2'] = jax.random.normal(next(it), (D_MODEL // 4, len(KV_OPTS)), jnp.float32) * s
        inp['r_b2'] = jnp.zeros((len(KV_OPTS),), jnp.float32)
        for i, nkv in enumerate(KV_OPTS):
            inp[f'wq{i}'] = jax.random.normal(next(it), (D_MODEL, D_MODEL), jnp.float32) * s
            inp[f'wk{i}'] = jax.random.normal(next(it), (D_MODEL, nkv * D_K), jnp.float32) * s
            inp[f'wv{i}'] = jax.random.normal(next(it), (D_MODEL, nkv * D_K), jnp.float32) * s
            inp[f'wo{i}'] = jax.random.normal(next(it), (D_MODEL, D_MODEL), jnp.float32) * s
        return inp
    _L3_ffn_all = _L3_ffn_setup()
    _L3_ffn_in = {k: v for k, v in _L3_ffn_all.items() if k in ('r_w1', 'r_b1', 'r_w2', 'r_b2', 'wq0', 'wk0', 'wv0', 'wo0', 'wq1', 'wk1', 'wv1', 'wo1', 'wq2', 'wk2', 'wv2', 'wo2')}
    del _L3_ffn_all
    return {'x': x, 'src': src, 'dst': dst, 'edge_type_32': edge_type_32, 'edge_weight': edge_weight, 'edge_weight1': edge_weight1, 'L0_gnn_weight': _L0_gnn_in['weight'], 'L0_gnn_bias': _L0_gnn_in['bias'], 'L0_ffn_Wg': _L0_ffn_in['Wg'], 'L0_ffn_bg': _L0_ffn_in['bg'], 'L0_ffn_We': _L0_ffn_in['We'], 'L0_ffn_be': _L0_ffn_in['be'], 'L1_gnn_W_conv': _L1_gnn_in['W_conv'], 'L1_gnn_b_conv': _L1_gnn_in['b_conv'], 'L1_gnn_W_lin': _L1_gnn_in['W_lin'], 'L1_gnn_b_lin': _L1_gnn_in['b_lin'], 'L1_ffn_gate_weight': _L1_ffn_in['gate_weight'], 'L1_ffn_experts': _L1_ffn_in['experts'], 'L2_gnn_bases': _L2_gnn_in['bases'], 'L2_gnn_w_comp': _L2_gnn_in['w_comp'], 'L2_gnn_h_bias': _L2_gnn_in['h_bias'], 'L2_ffn_W_ih': _L2_ffn_in['W_ih'], 'L2_ffn_W_hh': _L2_ffn_in['W_hh'], 'L2_ffn_b_ih': _L2_ffn_in['b_ih'], 'L2_ffn_b_hh': _L2_ffn_in['b_hh'], 'L2_ffn_W_sel': _L2_ffn_in['W_sel'], 'L2_ffn_b_sel': _L2_ffn_in['b_sel'], 'L3_gnn_W1': _L3_gnn_in['W1'], 'L3_gnn_att_src1': _L3_gnn_in['att_src1'], 'L3_gnn_att_dst1': _L3_gnn_in['att_dst1'], 'L3_gnn_b1': _L3_gnn_in['b1'], 'L3_gnn_W2': _L3_gnn_in['W2'], 'L3_gnn_att_src2': _L3_gnn_in['att_src2'], 'L3_gnn_att_dst2': _L3_gnn_in['att_dst2'], 'L3_gnn_b2': _L3_gnn_in['b2'], 'L3_gnn_fcW': _L3_gnn_in['fcW'], 'L3_gnn_fcb': _L3_gnn_in['fcb'], 'L3_ffn_r_w1': _L3_ffn_in['r_w1'], 'L3_ffn_r_b1': _L3_ffn_in['r_b1'], 'L3_ffn_r_w2': _L3_ffn_in['r_w2'], 'L3_ffn_r_b2': _L3_ffn_in['r_b2'], 'L3_ffn_wq0': _L3_ffn_in['wq0'], 'L3_ffn_wk0': _L3_ffn_in['wk0'], 'L3_ffn_wv0': _L3_ffn_in['wv0'], 'L3_ffn_wo0': _L3_ffn_in['wo0'], 'L3_ffn_wq1': _L3_ffn_in['wq1'], 'L3_ffn_wk1': _L3_ffn_in['wk1'], 'L3_ffn_wv1': _L3_ffn_in['wv1'], 'L3_ffn_wo1': _L3_ffn_in['wo1'], 'L3_ffn_wq2': _L3_ffn_in['wq2'], 'L3_ffn_wk2': _L3_ffn_in['wk2'], 'L3_ffn_wv2': _L3_ffn_in['wv2'], 'L3_ffn_wo2': _L3_ffn_in['wo2']}

def reference(x, src, dst, edge_type_32, edge_weight, edge_weight1, L0_gnn_weight, L0_gnn_bias, L0_ffn_Wg, L0_ffn_bg, L0_ffn_We, L0_ffn_be, L1_gnn_W_conv, L1_gnn_b_conv, L1_gnn_W_lin, L1_gnn_b_lin, L1_ffn_gate_weight, L1_ffn_experts, L2_gnn_bases, L2_gnn_w_comp, L2_gnn_h_bias, L2_ffn_W_ih, L2_ffn_W_hh, L2_ffn_b_ih, L2_ffn_b_hh, L2_ffn_W_sel, L2_ffn_b_sel, L3_gnn_W1, L3_gnn_att_src1, L3_gnn_att_dst1, L3_gnn_b1, L3_gnn_W2, L3_gnn_att_src2, L3_gnn_att_dst2, L3_gnn_b2, L3_gnn_fcW, L3_gnn_fcb, L3_ffn_r_w1, L3_ffn_r_b1, L3_ffn_r_w2, L3_ffn_r_b2, L3_ffn_wq0, L3_ffn_wk0, L3_ffn_wv0, L3_ffn_wo0, L3_ffn_wq1, L3_ffn_wk1, L3_ffn_wv1, L3_ffn_wo1, L3_ffn_wq2, L3_ffn_wk2, L3_ffn_wv2, L3_ffn_wo2):
    import jax
    import jax.numpy as jnp

    def _L0_gnn_ref(x, edge_index, weight, bias):
        import jax, jax.numpy as jnp
        import numpy as np
        N_NODES = 1250
        N_EDGES = 9375
        IN_C = 512
        OUT_C = 512
        K_INIT = 7

        def _spmm(row, col, lap, x, num_nodes):
            msgs = lap[:, None] * x[col]
            return jax.ops.segment_sum(msgs, row, num_segments=num_nodes)
        row, col = (edge_index[0], edge_index[1])
        num_nodes = x.shape[0]
        Kw = weight.shape[0]
        deg = jax.ops.segment_sum(jnp.ones_like(row, dtype=x.dtype), row, num_segments=num_nodes)
        dinv = jnp.where(deg > 0, jax.lax.rsqrt(jnp.maximum(deg, 1e-30)), 0.0)
        lap = -dinv[row] * dinv[col]
        Tx_0 = x
        out = Tx_0 @ weight[0]
        Tx_1 = _spmm(row, col, lap, x, num_nodes)
        out = out + Tx_1 @ weight[1]
        for k in range(2, Kw):
            Tx_2 = 2.0 * _spmm(row, col, lap, Tx_1, num_nodes) - Tx_0
            out = out + Tx_2 @ weight[k]
            Tx_0, Tx_1 = (Tx_1, Tx_2)
        return out + bias

    def _L0_ffn_ref(x, Wg, bg, We, be):
        import jax, jax.numpy as jnp
        import numpy as np
        B, S, D, E, O = (1024, 256, 512, 16, 512)
        scores = jax.nn.softmax(jnp.mean(x, axis=1) @ Wg + bg, axis=-1)
        idx = jnp.argmax(scores, axis=-1)
        gate = jnp.take_along_axis(scores, idx[:, None], axis=-1)
        W_sel = We[idx]
        b_sel = be[idx]
        y = jnp.einsum('bsd,bdo->bso', x, W_sel) + b_sel[:, None, :]
        return gate[:, :, None] * y

    def _L1_gnn_ref(x, edge_index, edge_weight, W_conv, b_conv, W_lin, b_lin):
        import jax, jax.numpy as jnp
        import numpy as np
        N = 3125
        E = 100000
        F_IN = 512
        H = 128
        n = x.shape[0]
        src, dst = (edge_index[0], edge_index[1])
        loop = jnp.arange(n, dtype=edge_index.dtype)
        src_f = jnp.concatenate([src, loop])
        dst_f = jnp.concatenate([dst, loop])
        w = jnp.concatenate([edge_weight, jnp.ones((n,), x.dtype)])
        deg = jax.ops.segment_sum(w, dst_f, num_segments=n)
        dinv = jnp.where(deg > 0, jax.lax.rsqrt(deg), 0.0)
        norm = dinv[src_f] * w * dinv[dst_f]
        h = x @ W_conv
        agg = jax.ops.segment_sum(h[src_f] * norm[:, None], dst_f, num_segments=n) + b_conv
        return agg @ W_lin + b_lin

    def _L1_ffn_ref(x, gate_weight, experts):
        import jax, jax.numpy as jnp
        import numpy as np
        EPS = 1e-06
        SINKHORN_ITERS = 8
        TEMPERATURE = 1.0
        B, N, D = (4, 512, 512)
        E, OUT = (8, 512)
        H = 1

        def _sinkhorn(logits):
            t = jnp.log(jnp.clip(logits, EPS)) / TEMPERATURE
            for _ in range(SINKHORN_ITERS):
                t = t - jax.nn.logsumexp(t, axis=-2, keepdims=True)
                t = t - jax.nn.logsumexp(t, axis=-1, keepdims=True)
            return jnp.exp(t)
        b, n, d = x.shape
        e = experts.shape[0]
        m = n // e
        xh = x[:, None, :, :]
        gate_logits = jnp.einsum('bhnd,hde->bhne', xh, gate_weight)
        gates = _sinkhorn(gate_logits)
        g_t = jnp.swapaxes(gates, -1, -2)
        vals, idx = jax.lax.top_k(g_t, m)
        gate_values = jnp.transpose(vals, (2, 0, 1, 3))[..., None]
        routed = jnp.take_along_axis(xh[:, :, None, :, :], idx[..., None], axis=3)
        routed = jnp.transpose(routed, (2, 0, 1, 3, 4))
        expert_w = experts[:, None, :, :]
        outputs = jnp.einsum('ebhmi,ehio->ebhmo', routed, expert_w)
        outputs = outputs * gate_values
        bh_idx = idx.reshape(b, 1, e * m)
        bh_vals = jnp.transpose(outputs, (1, 2, 0, 3, 4)).reshape(b, 1, e * m, outputs.shape[-1])

        def scat(i1, v1):
            return jnp.zeros((n, v1.shape[-1]), dtype=v1.dtype).at[i1].set(v1)
        routed_back = jax.vmap(jax.vmap(scat))(bh_idx, bh_vals)
        return routed_back[:, 0]

    def _L2_gnn_ref(x, bases, w_comp, h_bias, norm, src, dst, etype):
        import jax, jax.numpy as jnp
        import numpy as np
        N_NODES = 1250
        N_EDGES = 20000
        IN_FEAT = 512
        OUT_FEAT = 512
        NUM_RELS = 32
        NUM_BASES = 8
        n_nodes = x.shape[0]
        weight = jnp.einsum('rb,bio->rio', w_comp, bases)
        h_rel = jnp.einsum('ni,rio->rno', x, weight)
        msg = h_rel[etype, src] * norm
        out = jax.ops.segment_sum(msg, dst, num_segments=n_nodes)
        out = out + h_bias
        return out

    def _L2_ffn_ref(x, W_ih, W_hh, b_ih, b_hh, W_sel, b_sel):
        import jax, jax.numpy as jnp
        import numpy as np
        B, T, I, H, S = (64, 128, 512, 512, 4)

        def _lstm_activate(gates, c):
            i, f, g, o = jnp.split(gates, 4, axis=-1)
            c_new = jax.nn.sigmoid(f) * c + jax.nn.sigmoid(i) * jnp.tanh(g)
            h_new = jax.nn.sigmoid(o) * jnp.tanh(c_new)
            return (h_new, c_new)
        Bx, Tx, Ix = x.shape
        Sx, fourH, _ = W_ih.shape
        Hx = fourH // 4
        c0 = jnp.zeros((Bx, Hx), x.dtype)
        g0 = x[:, 0] @ W_ih[0].T + b_ih[0] + b_hh[0]
        h, c = _lstm_activate(g0, c0)

        def step(carry, x_t):
            h, c = carry
            sel_in = jnp.concatenate([h, c, x_t], axis=-1)
            logits = sel_in @ W_sel.T + b_sel
            onehot = jax.nn.one_hot(jnp.argmax(logits, axis=-1), Sx, dtype=x_t.dtype)
            g_all = jnp.einsum('bi,sgi->bsg', x_t, W_ih) + jnp.einsum('bh,sgh->bsg', h, W_hh) + b_ih + b_hh
            g = jnp.einsum('bsg,bs->bg', g_all, onehot)
            h2, c2 = _lstm_activate(g, c)
            return ((h2, c2), h2)
        xs = jnp.swapaxes(x[:, 1:], 0, 1)
        (_, _), hs = jax.lax.scan(step, (h, c), xs)
        outputs = jnp.concatenate([h[:, None], jnp.swapaxes(hs, 0, 1)], axis=1)
        return outputs

    def _L3_gnn_ref(x, edge_index, W1, att_src1, att_dst1, b1, W2, att_src2, att_dst2, b2, fcW, fcb):
        import jax, jax.numpy as jnp
        import numpy as np
        N_NODES = 625
        N_EDGES = 10000
        IN_DIM = 512
        HID = 256
        HEADS = 4
        OUT_DIM = 512
        NEG_SLOPE = 0.2

        def _glorot(key, shape):
            fan_in, fan_out = (shape[0], shape[-1])
            lim = jnp.sqrt(6.0 / (fan_in + fan_out))
            return jax.random.uniform(key, shape, jnp.float32, -lim, lim)

        def gat_conv(x, src, dst, W, att_src, att_dst, bias):
            N = x.shape[0]
            h = (x @ W).reshape(N, HEADS, HID)
            a_src = jnp.sum(h * att_src, axis=-1)
            a_dst = jnp.sum(h * att_dst, axis=-1)
            e = jax.nn.leaky_relu(a_src[src] + a_dst[dst], NEG_SLOPE)
            m = jax.ops.segment_max(e, dst, num_segments=N)
            e = jnp.exp(e - m[dst])
            s = jax.ops.segment_sum(e, dst, num_segments=N)
            alpha = e / (s[dst] + 1e-16)
            msg = alpha[:, :, None] * h[src]
            out = jax.ops.segment_sum(msg, dst, num_segments=N)
            return out.reshape(N, HEADS * HID) + bias
        N = x.shape[0]
        loops = jnp.arange(N, dtype=edge_index.dtype)
        src = jnp.concatenate([edge_index[0], loops])
        dst = jnp.concatenate([edge_index[1], loops])
        h = gat_conv(x, src, dst, W1, att_src1, att_dst1, b1)
        h = jax.nn.relu(h)
        h = gat_conv(h, src, dst, W2, att_src2, att_dst2, b2)
        h = jax.nn.relu(h)
        return h @ fcW + fcb

    def _L3_ffn_ref(x, r_w1, r_b1, r_w2, r_b2, wq0, wk0, wv0, wo0, wq1, wk1, wv1, wo1, wq2, wk2, wv2, wo2):
        import jax, jax.numpy as jnp
        import numpy as np
        D_MODEL = 512
        N_HEADS = 8
        KV_OPTS = (8, 4, 1)
        D_K = D_MODEL // N_HEADS

        def gqa(x, wq, wk, wv, wo, n_kv):
            B, S, _ = x.shape
            groups = N_HEADS // n_kv
            q = (x @ wq).reshape(B, S, N_HEADS, D_K).transpose(0, 2, 1, 3)
            k = (x @ wk).reshape(B, S, n_kv, D_K).transpose(0, 2, 1, 3)
            v = (x @ wv).reshape(B, S, n_kv, D_K).transpose(0, 2, 1, 3)
            k = jnp.repeat(k, groups, axis=1)
            v = jnp.repeat(v, groups, axis=1)
            scores = jnp.einsum('bhqd,bhkd->bhqk', q, k) / jnp.sqrt(jnp.float32(D_K))
            attn = jax.nn.softmax(scores, axis=-1)
            out = jnp.einsum('bhqk,bhkd->bhqd', attn, v)
            out = out.transpose(0, 2, 1, 3).reshape(B, S, D_MODEL)
            return out @ wo
        routing_input = x.mean(axis=1)
        logits = jax.nn.relu(routing_input @ r_w1 + r_b1) @ r_w2 + r_b2
        sel = jnp.argmax(jax.nn.softmax(logits, axis=-1), axis=-1)
        params = [(wq0, wk0, wv0, wo0), (wq1, wk1, wv1, wo1), (wq2, wk2, wv2, wo2)]
        out = jnp.zeros_like(x)
        for i, nkv in enumerate(KV_OPTS):
            yi = gqa(x, *params[i], nkv)
            mask = (sel == i)[:, None, None]
            out = jnp.where(mask, yi, out)
        return out
    edge_index = jnp.stack([src, dst])
    x = x + _L0_gnn_ref(_layernorm(x, axis=-1), edge_index, L0_gnn_weight, L0_gnn_bias)
    x = x + _L0_ffn_ref(_layernorm(x, axis=-1)[None], L0_ffn_Wg, L0_ffn_bg, L0_ffn_We, L0_ffn_be)[0]
    x = x + _L1_gnn_ref(_layernorm(x, axis=-1), edge_index, edge_weight, L1_gnn_W_conv, L1_gnn_b_conv, L1_gnn_W_lin, L1_gnn_b_lin)
    x = x + _L1_ffn_ref(_layernorm(x, axis=-1)[None], L1_ffn_gate_weight, L1_ffn_experts)[0]
    x = x + _L2_gnn_ref(_layernorm(x, axis=-1), L2_gnn_bases, L2_gnn_w_comp, L2_gnn_h_bias, edge_weight1, src, dst, edge_type_32)
    x = x + _L2_ffn_ref(_layernorm(x, axis=-1)[None], L2_ffn_W_ih, L2_ffn_W_hh, L2_ffn_b_ih, L2_ffn_b_hh, L2_ffn_W_sel, L2_ffn_b_sel)[0]
    x = x + _L3_gnn_ref(_layernorm(x, axis=-1), edge_index, L3_gnn_W1, L3_gnn_att_src1, L3_gnn_att_dst1, L3_gnn_b1, L3_gnn_W2, L3_gnn_att_src2, L3_gnn_att_dst2, L3_gnn_b2, L3_gnn_fcW, L3_gnn_fcb)
    x = x + _L3_ffn_ref(_layernorm(x, axis=-1)[None], L3_ffn_r_w1, L3_ffn_r_b1, L3_ffn_r_w2, L3_ffn_r_b2, L3_ffn_wq0, L3_ffn_wk0, L3_ffn_wv0, L3_ffn_wo0, L3_ffn_wq1, L3_ffn_wk1, L3_ffn_wv1, L3_ffn_wo1, L3_ffn_wq2, L3_ffn_wk2, L3_ffn_wv2, L3_ffn_wo2)[0]
    return x

_drawn_inputs = setup_inputs


def setup_inputs(seed=0):
    import zlib

    import numpy as np

    out = dict(_drawn_inputs(seed))
    spreads = {'L1_gnn_b_conv': (0.0, 0.1),
     'L1_gnn_b_lin': (0.0, 0.1),
     'L2_gnn_h_bias': (0.0, 0.1),
     'L3_gnn_b1': (0.0, 0.654),
     'L3_gnn_b2': (0.0, 0.394),
     'L3_gnn_fcb': (0.0, 0.275),
     'L3_ffn_r_b1': (0.0, 0.1),
     'L3_ffn_r_b2': (0.0, 0.67)}
    factors = {'L0_gnn_bias': 2.68,
     'L0_ffn_be': 8.0,
     'L2_ffn_b_ih': 8.0,
     'L2_ffn_b_hh': 4.602,
     'L2_ffn_b_sel': 3.999,
     'L3_gnn_W1': 4.082,
     'L3_gnn_att_src1': 6.665,
     'L3_gnn_att_dst1': 8.0,
     'L3_gnn_att_src2': 8.0,
     'L3_gnn_att_dst2': 8.0,
     'L3_ffn_wq2': 8.0,
     'L3_ffn_wk2': 8.0,
     'L3_ffn_wv2': 6.73,
     'L3_ffn_wo2': 6.76}
    for name, (base, spread) in spreads.items():
        noise = np.random.default_rng([zlib.crc32(name.encode()), seed]).standard_normal(out[name].shape)
        drawn = base * np.exp(spread * noise) if base else spread * noise
        out[name] = jnp.asarray(drawn.astype(out[name].dtype))
    for name, factor in factors.items():
        out[name] = (out[name] * factor).astype(out[name].dtype)
    return out
```

```python
from contextlib import ExitStack

import concourse.bass as bass
from concourse import mybir
from concourse.alu_op_type import AluOpType as ALU

F32 = mybir.dt.float32
F16 = mybir.dt.float16
BF16 = mybir.dt.bfloat16
U32 = mybir.dt.uint32
I32 = mybir.dt.int32
ACT = mybir.ActivationFunctionType
X_AXIS = mybir.AxisListType.X
RMAX = bass.bass_isa.ReduceOp.absmax

N = 625
D = 512
R = 125
NT = N // R
KC = D // 128
E = 20000
ET = E // R
EPS = 1e-5
BIG = 1e30
WARM_PICK, WARM_GATES = 4, 4
H_SCALE = 1024.0


class Buffers:
    pass


def allocate(nc, ctx, I):
    B = Buffers()
    B.I = I

    def sb(name, shape, dt):
        return ctx.enter_context(nc.sbuf_tensor(name, shape, dt))

    def sem(name):
        return ctx.enter_context(nc.semaphore(name))

    B.x = sb("x", [R, NT, D], F32)
    B.xn_full = sb("xn", [128, NT * D], F32)
    B.xn = B.xn_full[0:R, :].rearrange("p (j d) -> p j d", j=NT)
    B.xnT = sb("xnT", [128, KC * N], F32)
    B.ident = sb("ident", [128, 128], F32)
    B.iota_h = sb("iota_h", [R, N], F16)
    B.iota_f = sb("iota_f", [R, N], F32)
    B.ones = sb("ones", [128, 128], F32)
    B.zero = sb("zero", [128, 512], BF16)
    B.srci = sb("srci", [R, ET], I32)
    B.w = sb("w", [R, ET], F32)
    B.srcf = sb("srcf", [R, ET], F32)
    B.dstf = sb("dstf", [R, ET], F32)
    B.cnt = sb("cnt", [R, NT, N], F32)
    B.wdeg = sb("wdeg", [R, NT], F32)
    B.stats = sb("ln_stats_sb", [R, NT, 6], F32)
    B.mv = sb("ln_mv", [R, NT, 2], F32)
    B.var = sb("ln_var_sb", [R, NT], F32)
    B.root = sb("ln_root", [R, NT], F32)
    B.rstd = sb("ln_rstd_sb", [R, NT], F32)
    B.bank = [ctx.enter_context(nc.psum_tensor(f"bank{i}", [128, 512], F32)) for i in range(8)]
    B.ln_stats, B.ln_aggr, B.ln_rstd, B.ln_norm, B.ln_turn, B.ln_xnT, B.ln_var, B.ln_sqrt = [
        sem(n) for n in ("ln_stats", "ln_aggr", "ln_rstd", "ln_norm", "ln_turn", "ln_xnT", "ln_var", "ln_sqrt")]
    B.ln_calls = 0
    return B


def load_constants(nc, B):
    I = B.I
    with ExitStack() as ctx:
        loaded = ctx.enter_context(nc.semaphore("const_loaded"))
        block = ctx.enter_context(nc.Block())

        @block.sync
        def _(sp):
            sp.dma_start(B.x[:], I["x"].rearrange("(j p) d -> p j d", p=R)).then_inc(loaded, 16)
            sp.dma_start(B.ident[:], I["c_ident"]).then_inc(loaded, 16)
            sp.wait_ge(loaded, 32)

        @block.vector
        def _(dve):
            nc.vector.memset(B.ones[:], 1.0)
            nc.vector.memset(B.zero[:], 0.0)

        @block.gpsimd
        def _(pool):
            nc.gpsimd.iota(B.iota_f[:], [[1, N]], base=0, channel_multiplier=0,
                           allow_small_or_imprecise_dtypes=True)
            nc.gpsimd.iota(B.iota_h[:], [[1, N]], base=0, channel_multiplier=0,
                           allow_small_or_imprecise_dtypes=True)


def inverse_root(nc, dve, out, v, root, step, base):
    nc.vector.reciprocal(out, root).then_inc(step, 1)
    dve.wait_ge(step, base + 1)
    nc.vector.tensor_tensor(root, out, out, ALU.mult).then_inc(step, 1)
    dve.wait_ge(step, base + 2)
    nc.vector.scalar_tensor_tensor(out=root, in0=root, scalar=-0.5, in1=v, op0=ALU.mult,
                                   op1=ALU.mult).then_inc(step, 1)
    dve.wait_ge(step, base + 3)
    nc.vector.scalar_tensor_tensor(out=out, in0=root, scalar=1.5, in1=out, op0=ALU.add,
                                   op1=ALU.mult).then_inc(step, 1)
    dve.wait_ge(step, base + 4)


def layernorm(nc, B):
    base = NT * B.ln_calls
    call = B.ln_calls
    B.ln_calls += 1
    with nc.Block() as block:
        @block.vector
        def _(dve):
            for j in range(NT):
                nc.vector.bn_stats(B.stats[:, j, :], B.x[:, j, :]).then_inc(B.ln_stats, 1)
            for j in range(NT):
                dve.wait_ge(B.ln_stats, base + j + 1)
                nc.vector.bn_aggr(B.mv[:, j, :], B.stats[:, j, :]).then_inc(B.ln_aggr, 1)
            dve.wait_ge(B.ln_aggr, base + NT)
            nc.vector.tensor_scalar(B.var[:], B.mv[:, :, 1], EPS, None, ALU.add).then_inc(B.ln_var, 1)
            dve.wait_ge(B.ln_sqrt, call + 1)
            inverse_root(nc, dve, B.rstd[:], B.var[:], B.root[:], B.ln_rstd, 4 * call)
            for j in range(NT):
                nc.vector.tensor_scalar(B.xn[:, j, :], B.x[:, j, :], B.mv[:, j, 0:1], B.rstd[:, j:j + 1],
                                        ALU.subtract, ALU.mult).then_inc(B.ln_norm, 1)

        @block.tensor
        def _(pe):
            for j in range(NT):
                pe.wait_ge(B.ln_norm, base + j + 1)
                for c in range(KC):
                    t = nc.tensor.transpose(B.bank[j][:, c * R:(c + 1) * R],
                                            B.xn[:, j, c * 128:(c + 1) * 128], B.ident[0:R, 0:R])
                t.then_inc(B.ln_turn, 1)

        @block.scalar
        def _(act):
            act.wait_ge(B.ln_var, call + 1)
            nc.scalar.activation(B.root[:], B.var[:], ACT.Sqrt).then_inc(B.ln_sqrt, 1)
            for j in range(NT):
                act.wait_ge(B.ln_turn, base + j + 1)
                nc.scalar.copy(B.xnT[:].rearrange("p (c n) -> p c n", c=KC)[:, :, j * R:(j + 1) * R],
                               B.bank[j][:, 0:KC * R].rearrange("p (c n) -> p c n", c=KC)).then_inc(B.ln_xnT, 1)


def count_edges(nc, ctx, B):
    I = B.I

    def sb(name, shape, dt):
        return here.enter_context(nc.sbuf_tensor(name, shape, dt))

    def sem(name):
        return nc.alloc_semaphore(name)

    (loaded, cast, wsplit, hot_ready, hot_used, wcols, done) = [
        sem("cnt_" + n) for n in "loaded cast wsplit hot_ready hot_used wcols done".split()]
    evac = sem("cnt_evac")
    S = N + 3
    TAIL = S - 512
    with ExitStack() as here:
        dsti = sb("cnt_dsti", [R, ET], I32)
        rest = sb("cnt_rest", [R, ET], F32)
        w3 = sb("cnt_w3", [R, ET, 3], BF16)
        hot_d = sb("cnt_hot_d", [R, 2, N], BF16)
        hot_s = sb("cnt_hot_s", [R, 2, S], BF16)
        block = here.enter_context(nc.Block())

        def tail(m):
            return B.bank[5 + m // 3][0:R, (m % 3) * TAIL:(m % 3 + 1) * TAIL]

        @block.sync
        def _(sp):
            for dst, name in ((B.srci, "src"), (dsti, "dst"), (B.w, "edge_weight")):
                sp.dma_start(dst[:], I[name].rearrange("(p k) -> p k", p=R)).then_inc(loaded, 16)

        @block.vector
        def _(dve):
            dve.wait_ge(loaded, 48)
            nc.vector.tensor_copy(B.srcf[:], B.srci[:]).then_inc(cast, 1)
            nc.vector.tensor_copy(B.dstf[:], dsti[:]).then_inc(cast, 1)
            nc.vector.tensor_copy(w3[:, :, 0], B.w[:]).then_inc(wsplit, 1)
            dve.wait_ge(wsplit, 1)
            nc.vector.tensor_tensor(rest[:], B.w[:], w3[:, :, 0], ALU.subtract).then_inc(wsplit, 1)
            dve.wait_ge(wsplit, 2)
            nc.vector.tensor_copy(w3[:, :, 1], rest[:]).then_inc(wsplit, 1)
            dve.wait_ge(wsplit, 3)
            nc.vector.tensor_tensor(w3[:, :, 2], rest[:], w3[:, :, 1], ALU.subtract).then_inc(wsplit, 1)
            dve.wait_ge(wsplit, 4)
            dve.wait_ge(cast, 2)

            def hots(k, b):
                nc.vector.tensor_scalar(hot_d[:, b, :], B.iota_h[:], B.dstf[:, bass.ds(k, 1)], None,
                                        ALU.is_equal).then_inc(hot_ready, 1)
                nc.vector.tensor_scalar(hot_s[:, b, 0:N], B.iota_h[:], B.srcf[:, bass.ds(k, 1)], None,
                                        ALU.is_equal).then_inc(hot_ready, 1)
                nc.vector.tensor_copy(hot_s[:, b, N:S], w3[:, bass.ds(k, 1), :]).then_inc(hot_ready, 1)

            hots(0, 0)
            hots(1, 1)
            with dve.Fori(1, ET // 2) as pair:
                for b in range(2):
                    k = 2 * pair
                    dve.wait_ge(hot_used, k + b - 1)
                    hots(k + b, b)
            dve.wait_ge(done, 1)
            for m in range(NT):
                nc.vector.tensor_copy(B.cnt[:, m, 0:512], B.bank[m][0:R, :]).then_inc(evac, 1)
                nc.vector.tensor_copy(B.cnt[:, m, 512:N], tail(m)[:, 0:N - 512]).then_inc(evac, 1)
                nc.vector.tensor_reduce(B.wdeg[:, m:m + 1], tail(m)[:, N - 512:TAIL], X_AXIS, ALU.add).then_inc(evac, 1)

        @block.tensor
        def _(pe):
            for i in range(7):
                nc.tensor.matmul(B.bank[i][0:R, :], B.zero[0:R, 0:R], B.zero[0:R, :], start=True, stop=False)

            def add(k, b):
                pe.wait_ge(hot_ready, 3 * k + 3)
                for m in range(NT):
                    hd = hot_d[:, b, m * R:(m + 1) * R]
                    nc.tensor.matmul(B.bank[m][0:R, :], hd, hot_s[:, b, 0:512], start=False, stop=False)
                    t = nc.tensor.matmul(tail(m), hd, hot_s[:, b, 512:S], start=False, stop=False)
                t.then_inc(hot_used, 1)

            with pe.Fori(0, ET // 2) as pair:
                for b in range(2):
                    add(2 * pair + b, b)
            for i in range(7):
                t = nc.tensor.matmul(B.bank[i][0:R, :], B.zero[0:R, 0:R], B.zero[0:R, :], start=False, stop=True)
            t.then_inc(done, 1)


def chebyshev(nc, ctx, B):
    I = B.I
    K = I["L0_gnn_weight"].shape[0]

    def sb(name, shape, dt):
        return here.enter_context(nc.sbuf_tensor(name, shape, dt))

    def sem(name):
        return nc.alloc_semaphore(name)

    (w_loaded0, w_loaded1, bias_loaded, deg_done, dinv_step, row_done, lap_step, xw_done, prod_done, b_ready,
     half_ready, w_used, fin, root_done, rsqrt_step) = [sem("cheb_" + n) for n in (
         "w_loaded0 w_loaded1 bias_loaded deg_done dinv_step row_done lap_step xw_done prod_done b_ready "
         "half_ready w_used fin root_done rsqrt_step").split()]
    w_loaded = (w_loaded0, w_loaded1)
    xnT = B.xnT[:].rearrange("p (c n) -> p c n", c=KC)
    with ExitStack() as here:
        wk = sb("cheb_w", [128, 2, KC, D], F32)
        bias = sb("cheb_bias", [1, D], F32)
        lap = sb("cheb_lap", [R, NT, N], F32)
        deg = sb("cheb_deg", [R, NT], F32)
        root = sb("cheb_root", [R, NT], F32)
        has = sb("cheb_has", [R, NT], F32)
        dinv = sb("cheb_dinv", [R, NT], F32)
        dinv_cols = sb("cheb_dinv_cols", [R, NT, R], F32)
        bk = sb("cheb_b", [R, 3, NT, D], F32)
        half = sb("cheb_half", [R, NT, D], F32)
        block = here.enter_context(nc.Block())

        @block.sync
        def _(sp):
            sp.dma_start(bias[:], I["L0_gnn_bias"].rearrange("(a d) -> a d", a=1)).then_inc(bias_loaded, 16)
            for i, k in enumerate(reversed(range(K))):
                if i >= 2:
                    sp.wait_ge(w_used, i - 1)
                sp.dma_start(wk[:, i % 2], I["L0_gnn_weight"][k].rearrange("(c p) n -> p c n", p=128)
                             ).then_inc(w_loaded[i % 2], 16)

        @block.vector
        def _(dve):
            dve.wait_ge(deg_done, 1)
            nc.vector.tensor_copy(deg[:], B.bank[7][0:R, 0:NT]).then_inc(dinv_step, 1)
            dve.wait_ge(dinv_step, 1)
            nc.vector.tensor_scalar(has[:], deg[:], 0.0, None, ALU.is_gt).then_inc(dinv_step, 1)
            nc.vector.tensor_scalar(deg[:], deg[:], 1e-30, None, ALU.max).then_inc(dinv_step, 1)
            dve.wait_ge(dinv_step, 3)
            dve.wait_ge(root_done, 1)
            inverse_root(nc, dve, dinv[:], deg[:], root[:], rsqrt_step, 0)
            nc.vector.tensor_tensor(dinv[:], dinv[:], has[:], ALU.mult).then_inc(dinv_step, 1)
            dve.wait_ge(dinv_step, 4)
            for m in range(NT):
                nc.vector.tensor_scalar(dinv_cols[:, m, :], B.ones[0:R, 0:R], dinv[:, m:m + 1], None,
                                        ALU.mult).then_inc(dinv_step, 1)
            dve.wait_ge(row_done, 1)
            for m in range(NT):
                nc.vector.tensor_scalar(lap[:, m, :], B.cnt[:, m, :], dinv[:, m:m + 1], -2.0,
                                        ALU.mult, ALU.mult).then_inc(lap_step, 1)
            for m in range(NT):
                dve.wait_ge(lap_step, m + 1)
                nc.vector.tensor_tensor(lap[:, m, 0:500], lap[:, m, 0:500], B.bank[6][0:R, 0:500],
                                        ALU.mult).then_inc(lap_step, 1)
                nc.vector.tensor_tensor(lap[:, m, 500:N], lap[:, m, 500:N], B.bank[5][0:R, 0:R],
                                        ALU.mult).then_inc(lap_step, 1)
            n = 0
            for k in reversed(range(K)):
                for m in range(NT):
                    n += 1
                    dve.wait_ge(prod_done, n)
                    p = B.bank[m][0:R, :]
                    if k == 0:
                        nc.vector.tensor_tensor(bk[:, 0, m, :], p, bk[:, 2, m, :], ALU.subtract).then_inc(fin, 1)
                    elif k >= K - 2:
                        nc.vector.tensor_copy(bk[:, k % 3, m, :], p).then_inc(b_ready, 1)
                    else:
                        dve.wait_ge(b_ready, NT * (K - 1 - k) + m)
                        nc.vector.tensor_tensor(bk[:, k % 3, m, :], p, bk[:, (k + 2) % 3, m, :],
                                                ALU.subtract).then_inc(b_ready, 1)
                if k == 1:
                    for m in range(NT):
                        dve.wait_ge(b_ready, NT * (K - 2) + m + 1)
                        nc.vector.tensor_scalar(half[:, m, :], bk[:, 1, m, :], 0.5, None,
                                                ALU.mult).then_inc(half_ready, 1)
            for m in range(NT):
                dve.wait_ge(fin, m + 1)
                nc.vector.tensor_tensor(B.x[:, m, :], B.x[:, m, :], bk[:, 0, m, :], ALU.add).then_inc(fin, 1)

        @block.scalar
        def _(act):
            act.wait_ge(dinv_step, 3)
            nc.scalar.activation(root[:], deg[:], ACT.Sqrt).then_inc(root_done, 1)

        @block.tensor
        def _(pe):
            for m in range(NT):
                for t in range(NT):
                    last = nc.tensor.matmul(B.bank[7][0:R, m:m + 1], B.cnt[:, t, m * R:(m + 1) * R],
                                            B.ones[0:R, 0:1], start=(t == 0), stop=(t == NT - 1))
            last.then_inc(deg_done, 1)
            pe.wait_ge(dinv_step, 4 + NT)
            for m in range(NT):
                o = B.bank[6][0:R, m * R:(m + 1) * R] if m < 4 else B.bank[5][0:R, 0:R]
                last = nc.tensor.matmul(o, dinv_cols[:, m, :], B.ident[0:R, 0:R], start=True, stop=True)
            last.then_inc(row_done, 1)
            pe.wait_ge(bias_loaded, 16)
            n = 0
            for i, k in enumerate(reversed(range(K))):
                pe.wait_ge(w_loaded[i % 2], 16 * (i // 2 + 1))
                for m in range(NT):
                    if i > 0:
                        pe.wait_ge(b_ready, NT * (i - 1) + m + 1)
                    o = B.bank[m][0:R, :]
                    if k == 0:
                        nc.tensor.matmul(o, B.ones[0:1, 0:R], bias[:], start=True, stop=False)
                    for c in range(KC):
                        last = nc.tensor.matmul(o, xnT[:, c, m * R:(m + 1) * R], wk[:, i % 2, c, :],
                                                start=(c == 0 and k > 0), stop=(c == KC - 1 and i == 0))
                    if i == 0:
                        last.then_inc(prod_done, 1)
                last = nc.tensor.matmul(B.bank[7][0:1, 0:1], B.ones[0:1, 0:1], B.ones[0:1, 0:1],
                                        start=True, stop=True)
                last.then_inc(w_used, 1)
                if i == 0:
                    pe.wait_ge(lap_step, 3 * NT)
                    continue
                if k == 0:
                    pe.wait_ge(half_ready, NT)
                else:
                    pe.wait_ge(b_ready, NT * i)
                for m in range(NT):
                    for t in range(NT):
                        b = half[:, t, :] if k == 0 else bk[:, (k + 1) % 3, t, :]
                        last = nc.tensor.matmul(B.bank[m][0:R, :], lap[:, t, m * R:(m + 1) * R], b,
                                                start=False, stop=(t == NT - 1))
                    last.then_inc(prod_done, 1)


def route_expert(nc, ctx, B):
    I = B.I
    EX = I["L0_ffn_Wg"].shape[1]

    def sb(name, shape, dt):
        return here.enter_context(nc.sbuf_tensor(name, shape, dt))

    def sem(name):
        return nc.alloc_semaphore(name)

    (g_loaded, e_loaded, mean_ready, logit_done, top_step, exp_done, picked, gate_ready, gate_wide, gate_kept,
     prod_done) = [sem("route_" + n) for n in (
         "g_loaded e_loaded mean_ready logit_done top_step exp_done picked gate_ready gate_wide gate_kept "
         "prod_done").split()]
    xnT = B.xnT[:].rearrange("p (c n) -> p c n", c=KC)
    with ExitStack() as here:
        wg = sb("route_wg", [128, KC, EX], F32)
        bg = sb("route_bg", [1, EX], F32)
        we = sb("route_we", [128, KC, D], F32)
        be = sb("route_be", [1, D], F32)
        total = sb("route_total", [128, KC], F32)
        mean = sb("route_mean", [128, KC], F32)
        logit = sb("route_logit", [1, EX], F32)
        top = sb("route_top", [1, 8], F32)
        neg_top = sb("route_neg_top", [1, 1], F32)
        score = sb("route_score", [1, EX], F32)
        total_e = sb("route_total_e", [1, 1], F32)
        inv = sb("route_inv", [1, 1], F32)
        best = sb("route_best", [1, 8], F32)
        pick = sb("route_pick", [1, 8], U32)
        gate = sb("route_gate", [1, 1], F32)
        gates = sb("route_gates", [R, 1], F32)
        block = here.enter_context(nc.Block())

        @block.sync
        def _(sp):
            sp.dma_start(wg[:], I["L0_ffn_Wg"].rearrange("(c p) e -> p c e", p=128)).then_inc(g_loaded, 16)
            sp.dma_start(bg[:], I["L0_ffn_bg"].rearrange("(a e) -> a e", a=1)).then_inc(g_loaded, 16)
            sp.wait_ge(picked, 1)
            e = sp.value_load(pick[0:1, 0:1], min_val=0, max_val=EX - 1)
            sp.dma_start(we[:], I["L0_ffn_We"].rearrange("e (c p) n -> p (e c) n", p=128)[:, bass.ds(e * KC, KC), :]
                         ).then_inc(e_loaded, 16)
            sp.dma_start(be[:], I["L0_ffn_be"][bass.ds(e, 1), :]).then_inc(e_loaded, 16)

        @block.vector
        def _(dve):
            nc.vector.tensor_reduce(total[:], xnT, X_AXIS, ALU.add).then_inc(top_step, 1)
            dve.wait_ge(top_step, 1)
            nc.vector.tensor_scalar(mean[:], total[:], 1.0 / N, None, ALU.mult).then_inc(mean_ready, 1)
            dve.wait_ge(logit_done, 1)
            nc.vector.tensor_copy(logit[:], B.bank[0][0:1, 0:EX]).then_inc(top_step, 1)
            dve.wait_ge(top_step, 2)
            nc.vector.max(top[:], logit[:]).then_inc(top_step, 1)
            dve.wait_ge(top_step, 3)
            nc.vector.tensor_scalar(neg_top[:], top[:, 0:1], -1.0, None, ALU.mult).then_inc(top_step, 1)
            dve.wait_ge(exp_done, 1)
            nc.vector.reciprocal(inv[:], total_e[:]).then_inc(top_step, 1)
            nc.vector.max(best[:], score[:]).then_inc(top_step, 1)
            dve.wait_ge(top_step, 6)
            nc.vector.max_index(pick[:], best[:], score[:]).then_inc(picked, 1)
            nc.vector.tensor_tensor(gate[:], best[:, 0:1], inv[:], ALU.mult).then_inc(gate_ready, 1)
            dve.wait_ge(gate_wide, 1)
            nc.vector.tensor_copy(gates[:], B.bank[5][0:R, 0:1]).then_inc(gate_kept, 1)
            dve.wait_ge(gate_kept, 1)
            for m in range(NT):
                dve.wait_ge(prod_done, m + 1)
                nc.vector.scalar_tensor_tensor(out=B.x[:, m, :], in0=B.bank[m][0:R, :], scalar=gates[:, 0:1],
                                               in1=B.x[:, m, :], op0=ALU.mult, op1=ALU.add)

        @block.scalar
        def _(act):
            act.wait_ge(top_step, 4)
            nc.scalar.activation(score[:], logit[:], ACT.Exp, bias=neg_top[:], accum_out=total_e[:]
                                 ).then_inc(exp_done, 1)

        @block.tensor
        def _(pe):
            pe.wait_ge(g_loaded, 32)
            pe.wait_ge(mean_ready, 1)
            o = B.bank[0][0:1, 0:EX]
            nc.tensor.matmul(o, B.ones[0:1, 0:1], bg[:], start=True, stop=False)
            for c in range(KC):
                last = nc.tensor.matmul(o, mean[:, c:c + 1], wg[:, c, :], start=False, stop=(c == KC - 1))
            last.then_inc(logit_done, 1)
            pe.wait_ge(gate_ready, 1)
            nc.tensor.matmul(B.bank[5][0:R, 0:1], B.ones[0:1, 0:R], gate[:], start=True, stop=True
                             ).then_inc(gate_wide, 1)
            pe.wait_ge(e_loaded, 32)
            for m in range(NT):
                o = B.bank[m][0:R, :]
                nc.tensor.matmul(o, B.ones[0:1, 0:R], be[:], start=True, stop=False)
                for c in range(KC):
                    last = nc.tensor.matmul(o, xnT[:, c, m * R:(m + 1) * R], we[:, c, :], start=False,
                                            stop=(c == KC - 1))
                last.then_inc(prod_done, 1)


SLOTS = 16
LOT = 4
AHEAD = 2


def gcn(nc, ctx, B):
    I = B.I
    H = I["L1_gnn_W_conv"].shape[1]

    def sb(name, shape, dt):
        return here.enter_context(nc.sbuf_tensor(name, shape, dt))

    def sem(name):
        return nc.alloc_semaphore(name)

    (loaded, deg_step, root_done, rsqrt_step, h_done, h_scaled, h_stored, idx_kept, hot_ready,
     hot_used, agg_done, agg_kept, bias_ready, bias_done, out_done) = [sem("gcn_" + n) for n in (
         "loaded deg_step root_done rsqrt_step h_done h_scaled h_stored idx_kept hot_ready "
         "hot_used agg_done agg_kept bias_ready bias_done out_done").split()]
    gathered = [sem(f"gcn_gathered{i}") for i in range(SLOTS)]
    idx_ready = [sem(f"gcn_idx_ready{i}") for i in range(SLOTS // LOT)]
    h_dram = nc.dram_tensor("gcn_h_rows", (N, H), F32, kind="Internal").ap()
    xnT = B.xnT[:].rearrange("p (c n) -> p c n", c=KC)
    with ExitStack() as here:
        wc = sb("gcn_wc", [128, KC, H], F32)
        wl = sb("gcn_wl", [H, D], F32)
        bc = sb("gcn_bc", [H, 1], F32)
        bl = sb("gcn_bl", [1, D], F32)
        bc_wide = sb("gcn_bc_wide", [H, R], F32)
        deg = sb("gcn_deg", [R, NT], F32)
        has = sb("gcn_has", [R, NT], F32)
        root = sb("gcn_root", [R, NT], F32)
        dinv = sb("gcn_dinv", [R, NT], F32)
        h = sb("gcn_h", [R, NT, H], F32)
        idx_all = sb("gcn_idx_all", [R, ET + AHEAD * LOT], I32)
        idx = sb("gcn_idx", [R, SLOTS], I32)
        rows = sb("gcn_rows", [R, SLOTS, H], F32)
        hot = sb("gcn_hot", [R, 2, N], F32)
        aggT = sb("gcn_aggT", [H, N], F32)
        block = here.enter_context(nc.Block())

        @block.sync
        def _(sp):
            sp.dma_start(wc[:], I["L1_gnn_W_conv"].rearrange("(c p) h -> p c h", p=128)).then_inc(loaded, 16)
            sp.dma_start(wl[:], I["L1_gnn_W_lin"]).then_inc(loaded, 16)
            sp.dma_start(bc[:], I["L1_gnn_b_conv"].rearrange("(h a) -> h a", a=1)).then_inc(loaded, 16)
            sp.dma_start(bl[:], I["L1_gnn_b_lin"].rearrange("(a d) -> a d", a=1)).then_inc(loaded, 16)
            sp.wait_ge(h_scaled, NT)
            sp.dma_start(h_dram.rearrange("(j p) h -> p j h", p=R), h[:]).then_inc(h_stored, 16)

        @block.gpsimd
        def _(pool):
            pool.wait_ge(h_stored, 16)
            with pool.Fori(1, ET // SLOTS + 1) as g:
                for i in range(SLOTS):
                    if i % LOT == 0:
                        pool.wait_ge(h_stored, 16)
                        pool.wait_ge(idx_ready[i // LOT], g)
                    nc.gpsimd.indirect_dma_start(
                        out=rows[:, i, :], out_offset=None, in_=h_dram,
                        in_offset=bass.IndirectOffsetOnAxis(ap=idx[:, i:i + 1], axis=0)
                    ).then_inc(gathered[i], 16)

        @block.vector
        def _(dve):
            nc.vector.memset(idx_all[:, ET:ET + AHEAD * LOT], 0).then_inc(idx_kept, 1)
            nc.vector.tensor_copy(idx_all[:, 0:ET], B.srci[:]).then_inc(idx_kept, 1)
            nc.vector.tensor_scalar(deg[:], B.wdeg[:], 1.0, None, ALU.add).then_inc(deg_step, 1)
            dve.wait_ge(deg_step, 1)
            nc.vector.tensor_scalar(has[:], deg[:], 0.0, None, ALU.is_gt).then_inc(deg_step, 1)
            nc.vector.tensor_scalar(deg[:], deg[:], 1e-30, None, ALU.max).then_inc(deg_step, 1)
            dve.wait_ge(root_done, 1)
            inverse_root(nc, dve, dinv[:], deg[:], root[:], rsqrt_step, 0)
            nc.vector.tensor_tensor(dinv[:], dinv[:], has[:], ALU.mult).then_inc(deg_step, 1)
            dve.wait_ge(deg_step, 4)
            for m in range(NT):
                dve.wait_ge(h_done, m + 1)
                nc.vector.tensor_scalar(h[:, m, :], B.bank[2 + m][0:R, 0:H], dinv[:, m:m + 1], None,
                                        ALU.mult).then_inc(h_scaled, 1)

            def hots(k, b):
                nc.vector.tensor_scalar(hot[:, b, :], B.iota_f[:], B.dstf[:, bass.ds(k, 1)],
                                        B.w[:, bass.ds(k, 1)], ALU.is_equal, ALU.mult).then_inc(hot_ready, 1)

            dve.wait_ge(idx_kept, 2)
            for i in range(AHEAD):
                nc.vector.tensor_copy(idx[:, i * LOT:(i + 1) * LOT], idx_all[:, i * LOT:(i + 1) * LOT]
                                      ).then_inc(idx_ready[i], 1)
            with dve.Fori(0, ET // SLOTS) as g:
                for i in range(SLOTS):
                    k = g * SLOTS + i
                    dve.wait_ge(hot_used, k + 1)
                    if i % LOT == 0:
                        at = (i + AHEAD * LOT) % SLOTS
                        nc.vector.tensor_copy(idx[:, at:at + LOT], idx_all[:, bass.ds(k + AHEAD * LOT, LOT)]
                                              ).then_inc(idx_ready[at // LOT], 1)
                    hots(k, i % 2)
            dve.wait_ge(agg_done, 1)
            nc.vector.tensor_copy(aggT[:, 0:500], B.bank[0][0:H, 0:500]).then_inc(agg_kept, 1)
            nc.vector.tensor_copy(aggT[:, 500:N], B.bank[1][0:H, 0:R]).then_inc(agg_kept, 1)
            nc.vector.tensor_scalar(bc_wide[:], B.ones[0:H, 0:R], bc[:, 0:1], None, ALU.mult).then_inc(bias_ready, 1)
            for m in range(NT):
                dve.wait_ge(out_done, m + 1)
                nc.vector.scalar_tensor_tensor(out=B.x[:, m, :], in0=B.bank[2 + m][0:R, :],
                                               scalar=dinv[:, m:m + 1], in1=B.x[:, m, :], op0=ALU.mult,
                                               op1=ALU.add).then_inc(deg_step, 1)
            dve.wait_ge(bias_done, 1)
            dve.wait_ge(deg_step, 4 + NT)
            for m in range(NT):
                nc.vector.tensor_tensor(B.x[:, m, :], B.x[:, m, :], B.bank[7][0:R, :], ALU.add)

        @block.scalar
        def _(act):
            act.wait_ge(deg_step, 3)
            nc.scalar.activation(root[:], deg[:], ACT.Sqrt).then_inc(root_done, 1)

        @block.tensor
        def _(pe):
            pe.wait_ge(loaded, 64)
            for m in range(NT):
                for c in range(KC):
                    last = nc.tensor.matmul(B.bank[2 + m][0:R, 0:H], xnT[:, c, m * R:(m + 1) * R], wc[:, c, :],
                                            start=(c == 0), stop=(c == KC - 1))
                last.then_inc(h_done, 1)
            for i in range(2):
                last = nc.tensor.matmul(B.bank[i][0:H, :], B.zero[:, 0:H], B.zero[:], start=True, stop=False)
            last.then_inc(hot_used, 2)
            pe.wait_ge(h_scaled, NT)
            for m in range(NT):
                o = B.bank[0][0:H, m * R:(m + 1) * R] if m < 4 else B.bank[1][0:H, 0:R]
                nc.tensor.matmul(o, h[:, m, :], B.ident[0:R, 0:R], start=False, stop=False)
            with pe.Fori(0, ET // SLOTS) as g:
                for i in range(SLOTS):
                    pe.wait_ge(gathered[i], (g + 1) * 16)
                    pe.wait_ge(hot_ready, g * SLOTS + i + 1)
                    nc.tensor.matmul(B.bank[0][0:H, 0:500], rows[:, i, :], hot[:, i % 2, 0:500], start=False,
                                     stop=False)
                    nc.tensor.matmul(B.bank[1][0:H, 0:R], rows[:, i, :], hot[:, i % 2, 500:N], start=False,
                                     stop=False).then_inc(hot_used, 1)
            for i in range(2):
                last = nc.tensor.matmul(B.bank[i][0:H, :], B.zero[:, 0:H], B.zero[:], start=False, stop=True)
            last.then_inc(agg_done, 1)
            pe.wait_ge(agg_kept, 2)
            for m in range(NT):
                nc.tensor.matmul(B.bank[2 + m][0:R, :], aggT[:, m * R:(m + 1) * R], wl[:], start=True, stop=True
                                 ).then_inc(out_done, 1)
            pe.wait_ge(bias_ready, 1)
            nc.tensor.matmul(B.bank[7][0:R, :], bc_wide[:], wl[:], start=True, stop=False)
            nc.tensor.matmul(B.bank[7][0:R, :], B.ones[0:1, 0:R], bl[:], start=False, stop=True
                             ).then_inc(bias_done, 1)


SINKHORN_ITERS = 8


def choose_experts(nc, ctx, B):
    I = B.I
    EX = I["L1_ffn_experts"].shape[0]
    ROUNDS = -(-(N // EX) // 8)
    SPARE = 8 * ROUNDS - N // EX

    def sb(name, shape, dt):
        return here.enter_context(nc.sbuf_tensor(name, shape, dt))

    def sem(name):
        return nc.alloc_semaphore(name)

    (g_loaded, w_loaded0, w_loaded1, logit_done, step, sum_done, gates_ready, gatesT_done, pick_step, taken_ready,
     taken_done, prod_done, added) = [sem("choose_" + n) for n in (
         "g_loaded w_loaded0 w_loaded1 logit_done step sum_done gates_ready gatesT_done pick_step taken_ready "
         "taken_done prod_done added").split()]
    w_loaded = (w_loaded0, w_loaded1)
    xnT = B.xnT[:].rearrange("p (c n) -> p c n", c=KC)
    with ExitStack() as here:
        wg = sb("choose_wg", [128, KC, EX], F32)
        we = sb("choose_we", [128, 2, KC, D], F32)
        gates = sb("choose_gates", [R, NT, EX], F32)
        by_e = sb("choose_by_e", [R, EX], F32)
        inv_e = sb("choose_inv_e", [R, EX], F32)
        by_n = sb("choose_by_n", [R, NT], F32)
        inv_n = sb("choose_inv_n", [R, NT], F32)
        left = sb("choose_left", [EX, N + SPARE], F32)
        top = sb("choose_top", [EX, 8], F32)
        taken = sb("choose_taken", [EX, N], F32)
        took = sb("choose_took", [R, NT, EX], F32)
        order = sb("choose_order", [R, NT, EX], F32)
        last_e = sb("choose_last_e", [R, NT], F32)
        coef = sb("choose_coef", [R, NT, EX], F32)
        block = here.enter_context(nc.Block())

        def over_n(ap):
            return ap.rearrange("p (a e) -> p a e", a=1).to_broadcast((R, NT, EX))

        def over_e(ap):
            return ap.rearrange("p (j a) -> p j a", a=1).to_broadcast((R, NT, EX))

        @block.sync
        def _(sp):
            sp.dma_start(wg[:], I["L1_ffn_gate_weight"].rearrange("a (c p) e -> p (a c) e", p=128)
                         ).then_inc(g_loaded, 16)
            for e in range(EX):
                if e >= 2:
                    sp.wait_ge(prod_done, NT * (e - 1))
                sp.dma_start(we[:, e % 2], I["L1_ffn_experts"][e].rearrange("(c p) n -> p c n", p=128)
                             ).then_inc(w_loaded[e % 2], 16)

        @block.vector
        def _(dve):
            dve.wait_ge(logit_done, 1)
            nc.vector.tensor_scalar(gates[:], B.bank[5][0:R, 0:NT * EX].rearrange("p (j e) -> p j e", j=NT),
                                    1e-6, None, ALU.max).then_inc(gates_ready, 1)
            n = 0
            for it in range(SINKHORN_ITERS):
                dve.wait_ge(sum_done, it + 1)
                nc.vector.tensor_reduce(by_e[:], B.bank[6][0:R, 0:NT * EX].rearrange("p (j e) -> p e j", j=NT),
                                        X_AXIS, ALU.add).then_inc(step, 1)
                dve.wait_ge(step, n + 1)
                nc.vector.reciprocal(inv_e[:], by_e[:]).then_inc(step, 1)
                dve.wait_ge(step, n + 2)
                nc.vector.tensor_tensor(gates[:], gates[:], over_n(inv_e[:]), ALU.mult).then_inc(step, 1)
                dve.wait_ge(step, n + 3)
                nc.vector.tensor_reduce(by_n[:], gates[:], X_AXIS, ALU.add).then_inc(step, 1)
                dve.wait_ge(step, n + 4)
                nc.vector.reciprocal(inv_n[:], by_n[:]).then_inc(step, 1)
                dve.wait_ge(step, n + 5)
                nc.vector.tensor_tensor(gates[:], gates[:], over_e(inv_n[:]), ALU.mult).then_inc(gates_ready, 1)
                n += 5
            nc.vector.memset(left[:, N:N + SPARE], 3e38).then_inc(pick_step, 1)
            dve.wait_ge(gatesT_done, 1)
            nc.vector.tensor_copy(left[:, 0:500], B.bank[0][0:EX, 0:500]).then_inc(pick_step, 1)
            nc.vector.tensor_copy(left[:, 500:N], B.bank[1][0:EX, 0:R]).then_inc(pick_step, 1)
            for r in range(ROUNDS):
                dve.wait_ge(pick_step, 3 + 2 * r)
                nc.vector.max(top[:], left[:]).then_inc(pick_step, 1)
                dve.wait_ge(pick_step, 4 + 2 * r)
                nc.vector.match_replace(left[:], top[:], left[:], -1.0).then_inc(pick_step, 1)
            dve.wait_ge(pick_step, 3 + 2 * ROUNDS)
            nc.vector.tensor_scalar(taken[:], left[:, 0:N], 0.0, None, ALU.is_lt).then_inc(taken_ready, 1)
            dve.wait_ge(taken_done, 1)
            n = 3 + 2 * ROUNDS
            nc.vector.tensor_copy(took[:], B.bank[2][0:R, 0:NT * EX].rearrange("p (j e) -> p j e", j=NT)
                                  ).then_inc(pick_step, 1)
            dve.wait_ge(pick_step, n + 1)
            nc.vector.tensor_tensor(order[:], took[:], over_n(B.iota_f[:, 1:EX + 1]), ALU.mult).then_inc(pick_step, 1)
            dve.wait_ge(pick_step, n + 2)
            nc.vector.tensor_reduce(last_e[:], order[:], X_AXIS, ALU.max).then_inc(pick_step, 1)
            dve.wait_ge(pick_step, n + 3)
            nc.vector.tensor_tensor(coef[:], order[:], over_e(last_e[:]), ALU.is_equal).then_inc(pick_step, 1)
            dve.wait_ge(pick_step, n + 4)
            nc.vector.tensor_tensor(coef[:], coef[:], took[:], ALU.mult).then_inc(pick_step, 1)
            dve.wait_ge(pick_step, n + 5)
            nc.vector.tensor_tensor(coef[:], coef[:], gates[:], ALU.mult).then_inc(pick_step, 1)
            dve.wait_ge(pick_step, n + 6)
            for e in range(EX):
                for m in range(NT):
                    i = e * NT + m
                    dve.wait_ge(prod_done, i + 1)
                    if e > 0:
                        dve.wait_ge(added, i - NT + 1)
                    nc.vector.scalar_tensor_tensor(out=B.x[:, m, :], in0=B.bank[i % 8][0:R, :],
                                                   scalar=coef[:, m, e:e + 1], in1=B.x[:, m, :],
                                                   op0=ALU.mult, op1=ALU.add).then_inc(added, 1)

        @block.tensor
        def _(pe):
            pe.wait_ge(g_loaded, 16)
            for m in range(NT):
                for c in range(KC):
                    last = nc.tensor.matmul(B.bank[5][0:R, m * EX:(m + 1) * EX], xnT[:, c, m * R:(m + 1) * R],
                                            wg[:, c, :], start=(c == 0), stop=(c == KC - 1))
            last.then_inc(logit_done, 1)
            for it in range(SINKHORN_ITERS):
                pe.wait_ge(gates_ready, it + 1)
                nc.tensor.matmul(B.bank[6][0:R, 0:NT * EX], B.ones[0:R, 0:R],
                                 gates[:].rearrange("p j e -> p (j e)"), start=True, stop=True
                                 ).then_inc(sum_done, 1)
            pe.wait_ge(gates_ready, SINKHORN_ITERS + 1)
            for m in range(NT):
                o = B.bank[0][0:EX, m * R:(m + 1) * R] if m < 4 else B.bank[1][0:EX, 0:R]
                last = nc.tensor.transpose(o, gates[:, m, :], B.ident[0:R, 0:R])
            last.then_inc(gatesT_done, 1)
            pe.wait_ge(taken_ready, 1)
            for m in range(NT):
                last = nc.tensor.transpose(B.bank[2][0:R, m * EX:(m + 1) * EX], taken[:, m * R:(m + 1) * R],
                                           B.ident[0:EX, 0:EX])
            last.then_inc(taken_done, 1)
            for e in range(EX):
                pe.wait_ge(w_loaded[e % 2], 16 * (e // 2 + 1))
                for m in range(NT):
                    i = e * NT + m
                    if i >= 8:
                        pe.wait_ge(added, i - 7)
                    elif i == 0:
                        pe.wait_ge(pick_step, 4 + 2 * ROUNDS)
                    for c in range(KC):
                        last = nc.tensor.matmul(B.bank[i % 8][0:R, :], xnT[:, c, m * R:(m + 1) * R],
                                                we[:, e % 2, c, :], start=(c == 0), stop=(c == KC - 1))
                    last.then_inc(prod_done, 1)


GROUP = 16


L2_BASES = 8


def relational(nc, ctx, B):
    with nc.sbuf_tensor("rel_largest", [128, L2_BASES + 2], F32) as largest:
        B.largest = largest
        relational_rows(nc, ctx, B)
        relational_sum(nc, ctx, B)


def relational_rows(nc, ctx, B):
    I = B.I
    NB = I["L2_gnn_bases"].shape[0]
    NR = I["c_w_compT"].shape[1]
    NG = N // GROUP
    QN = 128 // NR
    Q = GROUP // QN

    def sb(name, shape, dt):
        return here.enter_context(nc.sbuf_tensor(name, shape, dt))

    def sem(name):
        return nc.alloc_semaphore(name)

    (w_loaded0, w_loaded1, comp_loaded, mix_ready, z_done, z_kept_a, z_kept_v, z_loaded, h_done, h_kept_a,
     h_kept_v, last_kept, last_stored, base_looked) = [sem("rel_" + n) for n in (
         "w_loaded0 w_loaded1 comp_loaded mix_ready z_done z_kept_a z_kept_v z_loaded h_done h_kept_a "
         "h_kept_v last_kept last_stored base_looked").split()]
    w_loaded = (w_loaded0, w_loaded1)
    z_stored = [sem(f"rel_z_stored{i}") for i in range(2)]
    h_stored = [sem(f"rel_h_stored{i}") for i in range(3)]
    z_dram = nc.dram_tensor("rel_z", (NB, N, D), F32, kind="Internal").ap()
    B.rel_h = nc.dram_tensor("rel_h", (N * NR, D), F32, kind="Internal").ap()
    xnT = B.xnT[:].rearrange("p (c n) -> p c n", c=KC)
    with ExitStack() as here:
        wb = sb("rel_bases", [128, 2, KC, D], F32)
        z = sb("rel_z_sb", [R, 2, NT, D], F32)
        zg = sb("rel_zg", [128, NG, D], F32)
        z_last = sb("rel_z_last", [NB, D], F32)
        compT = sb("rel_compT", [NB, NR], F32)
        comp_rep = sb("rel_comp_rep", [128, NR], F32)
        same = sb("rel_same", [128, GROUP], F32)
        mix = sb("rel_mix", [128, GROUP, NR], F32)
        ho = sb("rel_h_sb", [128, 3, Q, D], F32)
        block = here.enter_context(nc.Block())

        @block.sync
        def _(sp):
            sp.dma_start(same[:], I["c_same16"]).then_inc(comp_loaded, 16)
            sp.dma_start(compT[:], I["c_w_compT"]).then_inc(comp_loaded, 16)
            for b in range(NB):
                sp.dma_start(comp_rep[b * GROUP:(b + 1) * GROUP, :],
                             I["c_w_compT"][b:b + 1, :].to_broadcast((GROUP, NR))).then_inc(comp_loaded, 16)
            for b in range(NB):
                if b >= 2:
                    sp.wait_ge(z_done, NT * (b - 1))
                    sp.wait_ge(base_looked, b)
                sp.dma_start(wb[:, b % 2], I["L2_gnn_bases"][b].rearrange("(c p) n -> p c n", p=128)
                             ).then_inc(w_loaded[b % 2], 16)
            for g in range(NG):
                i = g % 3
                sp.wait_ge(h_kept_a, g + 1)
                sp.wait_ge(h_kept_v, g + 1)
                sp.dma_start(B.rel_h[g * GROUP * NR:(g + 1) * GROUP * NR, :].rearrange("(q p) d -> p q d", p=128),
                             ho[:, i]).then_inc(h_stored[i], 16)
            sp.wait_ge(last_kept, 1)
            sp.dma_start(B.rel_h[NG * GROUP * NR:N * NR, :], z[0:NR, 0, 0, :]).then_inc(last_stored, 16)
            sp.wait_ge(last_stored, 16)
            for i in range(3):
                sp.wait_ge(h_stored[i], 16 * ((NG - 1 - i) // 3 + 1))

        @block.gpsimd
        def _(pool):
            for b in range(NB):
                pool.wait_ge(z_kept_a, 2 * (b + 1))
                pool.wait_ge(z_kept_v, 3 * (b + 1))
                pool.dma_start(z_dram[b].rearrange("(j p) d -> p j d", p=R), z[:, b % 2]).then_inc(z_stored[b % 2], 16)
                pool.wait_ge(z_stored[b % 2], 16 * (b // 2 + 1))
                pool.dma_start(zg[b * GROUP:(b + 1) * GROUP, :, :],
                               z_dram[b, 0:NG * GROUP, :].rearrange("(g n) d -> n g d", n=GROUP)
                               ).then_inc(z_loaded, 16)
            pool.dma_start(z_last[:], z_dram[:, NG * GROUP, :]).then_inc(z_loaded, 16)

        @block.vector
        def _(dve):
            nc.vector.memset(B.largest[:], 0.0).then_inc(base_looked, 1)
            dve.wait_ge(comp_loaded, 16 * (2 + NB))
            dve.wait_ge(base_looked, 1)
            nc.vector.tensor_reduce(B.largest[:, NB:NB + 1], comp_rep[:], X_AXIS, ALU.max, apply_absolute_value=True)
            nc.vector.tensor_tensor(mix[:], same[:].rearrange("p (i a) -> p i a", a=1).to_broadcast((128, GROUP, NR)),
                                    comp_rep[:].rearrange("p (a r) -> p a r", a=1).to_broadcast((128, GROUP, NR)),
                                    ALU.mult).then_inc(mix_ready, 1)
            for b in range(NB):
                dve.wait_ge(w_loaded[b % 2], 16 * (b // 2 + 1))
                nc.vector.tensor_reduce(B.largest[:, b:b + 1], wb[:, b % 2].rearrange("p c n -> p (c n)"), X_AXIS,
                                        ALU.max, apply_absolute_value=True).then_inc(base_looked, 1)
                if b >= 2:
                    dve.wait_ge(z_stored[b % 2], 16 * (b // 2))
                for m in range(0, NT, 2):
                    dve.wait_ge(z_done, NT * b + m + 1)
                    nc.vector.tensor_copy(z[:, b % 2, m, :], B.bank[(NT * b + m) % 8][0:R, :]).then_inc(z_kept_v, 1)
            for g in range(NG):
                if g >= 3:
                    dve.wait_ge(h_stored[g % 3], 16 * (g // 3))
                dve.wait_ge(h_done, 2 * g + 1)
                for q in (0, 1):
                    last = nc.vector.tensor_copy(ho[:, g % 3, q, :], B.bank[(g % 2) * Q + q][:])
                last.then_inc(h_kept_v, 1)
            dve.wait_ge(h_done, 2 * NG + 1)
            nc.vector.tensor_copy(z[0:NR, 0, 0, :], B.bank[(NG % 2) * Q][0:NR, :]).then_inc(last_kept, 1)

        @block.scalar
        def _(act):
            for b in range(NB):
                if b >= 2:
                    act.wait_ge(z_stored[b % 2], 16 * (b // 2))
                for m in range(1, NT, 2):
                    act.wait_ge(z_done, NT * b + m + 1)
                    nc.scalar.copy(z[:, b % 2, m, :], B.bank[(NT * b + m) % 8][0:R, :]).then_inc(z_kept_a, 1)
            for g in range(NG):
                if g >= 3:
                    act.wait_ge(h_stored[g % 3], 16 * (g // 3))
                act.wait_ge(h_done, 2 * g + 2)
                for q in (2, 3):
                    last = nc.scalar.copy(ho[:, g % 3, q, :], B.bank[(g % 2) * Q + q][:])
                last.then_inc(h_kept_a, 1)

        @block.tensor
        def _(pe):
            for b in range(NB):
                pe.wait_ge(w_loaded[b % 2], 16 * (b // 2 + 1))
                for m in range(NT):
                    i = NT * b + m
                    if i >= 8:
                        pb, pm = (i - 8) // NT, (i - 8) % NT
                        if pm % 2:
                            pe.wait_ge(z_kept_a, 2 * pb + pm // 2 + 1)
                        else:
                            pe.wait_ge(z_kept_v, 3 * pb + pm // 2 + 1)
                    for c in range(KC):
                        last = nc.tensor.matmul(B.bank[i % 8][0:R, :], xnT[:, c, m * R:(m + 1) * R],
                                                wb[:, b % 2, c, :], start=(c == 0), stop=(c == KC - 1))
                    last.then_inc(z_done, 1)
            pe.wait_ge(mix_ready, 1)
            pe.wait_ge(z_kept_a, 2 * NB)
            pe.wait_ge(z_kept_v, 3 * NB)
            pe.wait_ge(z_loaded, 16 * (NB + 1))
            for g in range(NG):
                if g >= 2:
                    pe.wait_ge(h_kept_v, g - 1)
                    pe.wait_ge(h_kept_a, g - 1)
                for q in range(Q):
                    last = nc.tensor.matmul(B.bank[(g % 2) * Q + q][:],
                                            mix[:, q * QN:(q + 1) * QN, :].rearrange("p i r -> p (i r)"),
                                            zg[:, g, :], start=True, stop=True)
                    if q % 2:
                        last.then_inc(h_done, 1)
            pe.wait_ge(h_kept_v, NG - 1)
            nc.tensor.matmul(B.bank[(NG % 2) * Q][0:NR, :], compT[:], z_last[:], start=True, stop=True
                             ).then_inc(h_done, 1)


BUFS = 4


def relational_sum(nc, ctx, B):
    I = B.I
    NR = I["c_w_compT"].shape[1]
    NB = L2_BASES

    def sb(name, shape, dt):
        return here.enter_context(nc.sbuf_tensor(name, shape, dt))

    def sem(name):
        return nc.alloc_semaphore(name)

    (loaded, idx_step, max_step, max_all, scale_step, norm_ready, hi_ready, lo_ready, hot_ready, used, bias_done,
     done) = [sem("sum_" + n) for n in (
         "loaded idx_step max_step max_all scale_step norm_ready hi_ready lo_ready hot_ready used bias_done "
         "done").split()]
    gathered = [sem(f"sum_gathered{i}") for i in range(SLOTS)]
    idx_ready = [sem(f"sum_idx_ready{i}") for i in range(SLOTS // LOT)]
    with ExitStack() as here:
        et = sb("sum_et", [R, ET], I32)
        norm = sb("sum_norm", [R, ET], F32)
        bias = sb("sum_bias", [1, D], F32)
        idxf = sb("sum_idxf", [R, ET], F32)
        idx_all = sb("sum_idx_all", [R, ET + AHEAD * LOT], I32)
        idx = sb("sum_idx", [R, SLOTS], I32)
        rows = sb("sum_rows", [R, SLOTS, D], F32)
        parts = sb("sum_parts", [R, BUFS, 2, D], F16)
        hot = sb("sum_hot", [R, BUFS, N], F16)
        mx = sb("sum_mx", [128, 3], F32)
        mxa = sb("sum_mxa", [128, 3], F32)
        bound = sb("sum_bound", [128, 1], F32)
        expo = sb("sum_expo", [128, 1], I32)
        code = sb("sum_code", [128, 2], I32)
        bits = sb("sum_bits", [128, 2], I32)
        scale, inv = bits[0:R, 0:1].bitcast(F32), bits[0:R, 1:2].bitcast(F32)
        block = here.enter_context(nc.Block())

        @block.sync
        def _(sp):
            sp.dma_start(et[:], I["edge_type_32"].rearrange("(p k) -> p k", p=R)).then_inc(loaded, 16)
            sp.dma_start(norm[:], I["edge_weight1"].rearrange("(p k) a -> p (k a)", p=R)).then_inc(loaded, 16)
            sp.dma_start(bias[:], I["L2_gnn_h_bias"].rearrange("(a d) -> a d", a=1)).then_inc(loaded, 16)

        @block.gpsimd
        def _(pool):
            pool.wait_ge(max_step, 4)
            nc.gpsimd.partition_all_reduce(mxa[:], mx[:], 128, RMAX).then_inc(max_all, 1)
            with pool.Fori(1, ET // SLOTS + 1) as g:
                for i in range(SLOTS):
                    if i % LOT == 0:
                        pool.wait_ge(loaded, 48)
                        pool.wait_ge(idx_ready[i // LOT], g)
                    nc.gpsimd.indirect_dma_start(
                        out=rows[:, i, :], out_offset=None, in_=B.rel_h,
                        in_offset=bass.IndirectOffsetOnAxis(ap=idx[:, i:i + 1], axis=0)
                    ).then_inc(gathered[i], 16)

        @block.vector
        def _(dve):
            nc.vector.memset(idx_all[:, ET:ET + AHEAD * LOT], 0).then_inc(idx_step, 1)
            dve.wait_ge(loaded, 48)
            nc.vector.tensor_copy(idxf[:], et[:]).then_inc(idx_step, 1)
            dve.wait_ge(idx_step, 2)
            nc.vector.scalar_tensor_tensor(out=idxf[:], in0=B.srcf[:], scalar=float(NR), in1=idxf[:],
                                           op0=ALU.mult, op1=ALU.add).then_inc(idx_step, 1)
            dve.wait_ge(idx_step, 3)
            nc.vector.tensor_copy(idx_all[:, 0:ET], idxf[:]).then_inc(idx_step, 1)
            dve.wait_ge(idx_step, 4)
            for i in range(AHEAD):
                nc.vector.tensor_copy(idx[:, i * LOT:(i + 1) * LOT], idx_all[:, i * LOT:(i + 1) * LOT]
                                      ).then_inc(idx_ready[i], 1)
            nc.vector.tensor_reduce(B.largest[0:R, NB + 1:NB + 2], norm[:], X_AXIS, ALU.max,
                                    apply_absolute_value=True).then_inc(max_step, 1)
            nc.vector.tensor_reduce(mx[:, 0:1], B.largest[:, 0:NB], X_AXIS, ALU.max).then_inc(max_step, 1)
            nc.vector.tensor_copy(mx[:, 1:2], B.largest[:, NB:NB + 1]).then_inc(max_step, 1)
            dve.wait_ge(max_step, 1)
            nc.vector.tensor_copy(mx[:, 2:3], B.largest[:, NB + 1:NB + 2]).then_inc(max_step, 1)
            dve.wait_ge(max_all, 1)
            nc.vector.scalar_tensor_tensor(out=bound[:], in0=mxa[:, 0:1], scalar=float(NB * D), in1=mxa[:, 1:2],
                                           op0=ALU.mult, op1=ALU.mult).then_inc(scale_step, 1)
            dve.wait_ge(scale_step, 1)
            nc.vector.tensor_tensor(bound[:], bound[:], mxa[:, 2:3], ALU.mult).then_inc(scale_step, 1)
            dve.wait_ge(scale_step, 2)
            nc.vector.tensor_scalar(expo[:], bound[:].bitcast(I32), 23, None, ALU.logical_shift_right
                                    ).then_inc(scale_step, 1)
            dve.wait_ge(scale_step, 3)
            nc.vector.tensor_scalar(expo[:], expo[:], 32, None, ALU.max).then_inc(scale_step, 1)
            dve.wait_ge(scale_step, 4)
            nc.vector.tensor_scalar(code[:, 0:1], expo[:], -1.0, 268.0, ALU.mult, ALU.add).then_inc(scale_step, 1)
            nc.vector.tensor_scalar(code[:, 1:2], expo[:], -14.0, None, ALU.add).then_inc(scale_step, 1)
            dve.wait_ge(scale_step, 6)
            nc.vector.tensor_scalar(bits[:], code[:], 23, None, ALU.logical_shift_left).then_inc(scale_step, 1)
            dve.wait_ge(scale_step, 7)
            nc.vector.tensor_scalar(norm[:], norm[:], scale, None, ALU.mult).then_inc(norm_ready, 1)
            dve.wait_ge(norm_ready, 1)
            with dve.Fori(0, ET // SLOTS) as g:
                for i in range(SLOTS):
                    k = dve.snap(g * SLOTS + i)
                    dve.wait_ge(used, k + 1)
                    if i % LOT == 0:
                        at = (i + AHEAD * LOT) % SLOTS
                        nc.vector.tensor_copy(idx[:, at:at + LOT], idx_all[:, bass.ds(k + AHEAD * LOT, LOT)]
                                              ).then_inc(idx_ready[at // LOT], 1)
                    nc.vector.tensor_scalar(hot[:, i % BUFS, :], B.iota_h[:], B.dstf[:, bass.ds(k, 1)], None,
                                            ALU.is_equal).then_inc(hot_ready, 1)
                    dve.wait_ge(hi_ready, k + 1)
                    nc.vector.scalar_tensor_tensor(out=parts[:, i % BUFS, 1, :], in0=rows[:, i, :],
                                                   scalar=norm[:, bass.ds(k, 1)], in1=parts[:, i % BUFS, 0, :],
                                                   op0=ALU.mult, op1=ALU.subtract).then_inc(lo_ready, 1)
            dve.wait_ge(bias_done, 1)
            for m in range(NT):
                nc.vector.tensor_tensor(B.x[:, m, :], B.x[:, m, :], B.bank[NT][0:R, :], ALU.add
                                        ).then_inc(scale_step, 1)
            for m in range(NT):
                dve.wait_ge(scale_step, 8 + m)
                dve.wait_ge(done, m + 1)
                nc.vector.scalar_tensor_tensor(out=B.x[:, m, :], in0=B.bank[m][0:R, :], scalar=inv, in1=B.x[:, m, :],
                                               op0=ALU.mult, op1=ALU.add)

        @block.scalar
        def _(act):
            act.wait_ge(norm_ready, 1)
            with act.Fori(0, ET // SLOTS) as g:
                for i in range(SLOTS):
                    k = act.snap(g * SLOTS + i)
                    free = act.snap(k + 1)
                    due = act.snap((g + 1) * 16)
                    act.wait_ge(norm_ready, 1)
                    act.wait_ge(used, free)
                    act.wait_ge(gathered[i], due)
                    nc.scalar.activation(parts[:, i % BUFS, 0, :], rows[:, i, :], ACT.Copy,
                                         scale=norm[:, bass.ds(k, 1)]).then_inc(hi_ready, 1)

        @block.tensor
        def _(pe):
            pe.wait_ge(loaded, 48)
            nc.tensor.matmul(B.bank[NT][0:R, :], B.ones[0:1, 0:R], bias[:], start=True, stop=True
                             ).then_inc(bias_done, 1)
            for m in range(NT):
                last = nc.tensor.matmul(B.bank[m][0:R, :], B.zero[0:R, 0:R], B.zero[0:R, :], start=True, stop=False)
            last.then_inc(used, BUFS)
            with pe.Fori(0, ET // SLOTS) as g:
                for i in range(SLOTS):
                    pe.wait_ge(lo_ready, g * SLOTS + i + 1)
                    pe.wait_ge(hot_ready, g * SLOTS + i + 1)
                    for m in range(NT):
                        for a in range(2):
                            last = nc.tensor.matmul(B.bank[m][0:R, :], hot[:, i % BUFS, m * R:(m + 1) * R],
                                                    parts[:, i % BUFS, a, :], start=False, stop=False)
                    last.then_inc(used, 1)
            for m in range(NT):
                nc.tensor.matmul(B.bank[m][0:R, :], B.zero[0:R, 0:R], B.zero[0:R, :], start=False, stop=True
                                 ).then_inc(done, 1)


STEPS = N
CELLS = 4
GC = D // 128 * 4
CHUNK = 25
RING = 3 * CHUNK


def lstm_inputs(nc, ctx, B):
    I = B.I

    def sb(name, shape, dt):
        return here.enter_context(nc.sbuf_tensor("xg_" + name, shape, dt))

    def sem(name):
        return nc.alloc_semaphore("xg_" + name)

    (b_loaded, bias_ready, done, kept_a, kept_v, lx_done, lx_kept, lx_stored) = [sem(n) for n in (
        "b_loaded bias_ready done kept_a kept_v lx_done lx_kept lx_stored").split()]
    w_loaded = [sem(f"w_loaded{i}") for i in range(2)]
    stored = [sem(f"stored{i}") for i in range(2)]
    B.xg = nc.dram_tensor("lstm_xg", (CELLS, 128, STEPS * GC), F32, kind="Internal").ap()
    B.lx = nc.dram_tensor("lstm_lx", (STEPS, CELLS), F32, kind="Internal").ap()
    xnT = B.xnT[:].rearrange("p (c n) -> p c n", c=KC)
    CUT = 313
    LOADS = 2 * CELLS
    with ExitStack() as here:
        w = sb("w", [128, 2, KC, GC // 2, 128], F32)
        b_ih = sb("b_ih", [128, CELLS * GC], F32)
        b_hh = sb("b_hh", [128, CELLS * GC], F32)
        ws = sb("ws", [128, KC, CELLS], F32)
        bs = sb("bs", [1, CELLS], F32)
        g = sb("g", [128, 2, STEPS, GC], F32)
        lx = sb("lx_sb", [R, NT, CELLS], F32)
        block = here.enter_context(nc.Block())

        @block.sync
        def _(sp):
            sp.dma_start(b_ih[:], I["c_b_ih"]).then_inc(b_loaded, 16)
            sp.dma_start(b_hh[:], I["c_b_hh"]).then_inc(b_loaded, 16)
            sp.dma_start(ws[:], I["c_w_sel_x"]).then_inc(b_loaded, 16)
            sp.dma_start(bs[:], I["L2_ffn_b_sel"].rearrange("(a s) -> a s", a=1)).then_inc(b_loaded, 16)
            for n in range(LOADS):
                if n >= 2:
                    sp.wait_ge(done, GC // 2 * (n - 1))
                sp.dma_start(w[:, n % 2], I["c_w_ih"][n // 2, :, :, n % 2]).then_inc(w_loaded[n % 2], 16)
            sp.wait_ge(lx_kept, 1)
            sp.dma_start(B.lx.rearrange("(j p) s -> p j s", p=R), lx[:]).then_inc(lx_stored, 16)
            sp.wait_ge(lx_stored, 16)

        @block.gpsimd
        def _(pool):
            for s in range(CELLS):
                pool.wait_ge(kept_a, GC * (s + 1))
                pool.wait_ge(kept_v, GC * (s + 1))
                pool.dma_start(B.xg[s], g[:, s % 2].rearrange("p t g -> p (t g)")).then_inc(stored[s % 2], 16)
            for i in range(2):
                pool.wait_ge(stored[i], 16 * (CELLS // 2))

        @block.vector
        def _(dve):
            dve.wait_ge(b_loaded, 64)
            nc.vector.tensor_tensor(b_ih[:], b_ih[:], b_hh[:], ALU.add).then_inc(bias_ready, 1)
            dve.wait_ge(bias_ready, 1)
            for s in range(CELLS):
                if s >= 2:
                    dve.wait_ge(stored[s % 2], 16 * (s // 2))
                for c in range(GC):
                    i = s * GC + c
                    dve.wait_ge(done, i + 1)
                    nc.vector.tensor_scalar(g[:, s % 2, CUT:STEPS, c], B.bank[2 * (i % 4) + 1][:, 0:STEPS - CUT],
                                            b_ih[:, i:i + 1], None, ALU.add).then_inc(kept_v, 1)
            dve.wait_ge(lx_done, 1)
            nc.vector.tensor_copy(lx[:], B.bank[0][0:R, 0:NT * CELLS].rearrange("p (j s) -> p j s", j=NT)
                                  ).then_inc(lx_kept, 1)

        @block.scalar
        def _(act):
            act.wait_ge(bias_ready, 1)
            for s in range(CELLS):
                if s >= 2:
                    act.wait_ge(stored[s % 2], 16 * (s // 2))
                for c in range(GC):
                    i = s * GC + c
                    act.wait_ge(done, i + 1)
                    nc.scalar.activation(g[:, s % 2, 0:CUT, c], B.bank[2 * (i % 4)][:, 0:CUT], ACT.Identity,
                                         bias=b_ih[:, i:i + 1]).then_inc(kept_a, 1)

        @block.tensor
        def _(pe):
            for i in range(CELLS * GC):
                n = i // (GC // 2)
                if i % (GC // 2) == 0:
                    pe.wait_ge(w_loaded[n % 2], 16 * (n // 2 + 1))
                if i >= 4:
                    pe.wait_ge(kept_a, i - 3)
                    pe.wait_ge(kept_v, i - 3)
                for c in range(KC):
                    wt = w[:, n % 2, c, i % (GC // 2), :]
                    nc.tensor.matmul(B.bank[2 * (i % 4)][:, 0:CUT], wt, xnT[:, c, 0:CUT], start=(c == 0),
                                     stop=(c == KC - 1))
                    last = nc.tensor.matmul(B.bank[2 * (i % 4) + 1][:, 0:N - CUT], wt, xnT[:, c, CUT:N],
                                            start=(c == 0), stop=(c == KC - 1))
                last.then_inc(done, 1)
            pe.wait_ge(b_loaded, 64)
            pe.wait_ge(kept_a, CELLS * GC)
            pe.wait_ge(kept_v, CELLS * GC)
            for m in range(NT):
                o = B.bank[0][0:R, m * CELLS:(m + 1) * CELLS]
                nc.tensor.matmul(o, B.ones[0:1, 0:R], bs[:], start=True, stop=False)
                for c in range(KC):
                    last = nc.tensor.matmul(o, xnT[:, c, m * R:(m + 1) * R], ws[:, c, :], start=False,
                                            stop=(c == KC - 1))
            last.then_inc(lx_done, 1)


BLOCKS = CELLS * KC * 4
SHIFT = 2


def lstm(nc, ctx, B):
    lstm_inputs(nc, ctx, B)
    with ExitStack() as here:
        def sb(name, shape, dt):
            return here.enter_context(nc.sbuf_tensor("lstm_" + name, shape, dt))

        L = Buffers()
        L.raw = sb("w", [128, BLOCKS + SHIFT, 512], F32)
        L.inv = sb("inv_scale", [128, 1], F32)
        L.wsel = sb("wsel", [128, CELLS, 8], F32)
        L.lx = B.xn_full[0:1, 0:STEPS * CELLS]
        L.h = B.xnT
        split_weights(nc, ctx, B, L)
        lstm_steps(nc, ctx, B, L)
        add_hidden(nc, ctx, B, L)


def split_weights(nc, ctx, B, L):
    I = B.I

    def sb(name, shape, dt):
        return here.enter_context(nc.sbuf_tensor("split_" + name, shape, dt))

    def sem(name):
        return nc.alloc_semaphore("split_" + name)

    (s_loaded, max_step, max_all, scale_step, scale_ready, hi_ready, lo_ready) = [sem(n) for n in (
        "s_loaded max_step max_all scale_step scale_ready hi_ready lo_ready").split()]
    w_loaded = [sem(f"w_loaded{s}") for s in range(CELLS)]
    PER = BLOCKS // CELLS
    parts = L.raw[:].bitcast(F16).rearrange("p n (a k) -> p n a k", a=2)
    with ExitStack() as here:
        mx = sb("mx", [128, CELLS], F32)
        mx1 = sb("mx1", [128, 1], F32)
        mxa = sb("mxa", [128, 1], F32)
        expo = sb("expo", [128, 1], I32)
        code = sb("code", [128, 2], I32)
        bits = sb("bits", [128, 2], I32)
        block = here.enter_context(nc.Block())
        scale = bits[:, 0:1].bitcast(F32)

        @block.sync
        def _(sp):
            for s in range(CELLS):
                sp.dma_start(L.raw[:, SHIFT + s * PER:SHIFT + (s + 1) * PER, :], I["c_w_hh"][s]
                             ).then_inc(w_loaded[s], 16)
            sp.dma_start(L.lx, B.lx.rearrange("(a t) s -> a (t s)", a=1)).then_inc(s_loaded, 16)
            sp.dma_start(L.wsel[:], I["c_w_sel_state"]).then_inc(s_loaded, 16)
            sp.wait_ge(s_loaded, 32)

        @block.vector
        def _(dve):
            for s in range(CELLS):
                dve.wait_ge(w_loaded[s], 16)
                nc.vector.tensor_reduce(mx[:, s:s + 1], L.raw[:, SHIFT + s * PER:SHIFT + (s + 1) * PER, :].rearrange(
                    "p n k -> p (n k)"), X_AXIS, ALU.max, apply_absolute_value=True).then_inc(max_step, 1)
            dve.wait_ge(max_step, CELLS)
            nc.vector.tensor_reduce(mx1[:], mx[:], X_AXIS, ALU.max).then_inc(max_step, 1)
            dve.wait_ge(max_all, 1)
            nc.vector.tensor_scalar(expo[:], mxa[:].bitcast(I32), 23, None, ALU.logical_shift_right
                                    ).then_inc(scale_step, 1)
            dve.wait_ge(scale_step, 1)
            nc.vector.tensor_scalar(expo[:], expo[:], 32, None, ALU.max).then_inc(scale_step, 1)
            dve.wait_ge(scale_step, 2)
            nc.vector.tensor_scalar(code[:, 0:1], expo[:], -1.0, 268.0, ALU.mult, ALU.add).then_inc(scale_step, 1)
            nc.vector.tensor_scalar(code[:, 1:2], expo[:], -24.0, None, ALU.add).then_inc(scale_step, 1)
            dve.wait_ge(scale_step, 4)
            nc.vector.tensor_scalar(bits[:], code[:], 23, None, ALU.logical_shift_left).then_inc(scale_ready, 1)
            dve.wait_ge(scale_ready, 1)
            nc.vector.tensor_copy(L.inv[:], bits[:, 1:2].bitcast(F32)).then_inc(scale_step, 1)
            for n in range(BLOCKS):
                dve.wait_ge(hi_ready, n + 1)
                nc.vector.scalar_tensor_tensor(out=parts[:, n, 1, :], in0=L.raw[:, n + SHIFT, :], scalar=scale,
                                               in1=parts[:, n, 0, :], op0=ALU.mult, op1=ALU.subtract
                                               ).then_inc(lo_ready, 1)

        @block.gpsimd
        def _(pool):
            pool.wait_ge(max_step, CELLS + 1)
            nc.gpsimd.partition_all_reduce(mxa[:], mx1[:], 128, RMAX).then_inc(max_all, 1)

        @block.scalar
        def _(act):
            act.wait_ge(scale_ready, 1)
            for n in range(BLOCKS):
                if n >= SHIFT:
                    act.wait_ge(lo_ready, n - SHIFT + 1)
                nc.scalar.activation(parts[:, n, 0, :], L.raw[:, n + SHIFT, :], ACT.Copy, scale=scale
                                     ).then_inc(hi_ready, 1)


def lstm_steps(nc, ctx, B, L):
    def sb(name, shape, dt):
        return here.enter_context(nc.sbuf_tensor("step_" + name, shape, dt))

    def sem(name):
        return nc.alloc_semaphore("step_" + name)

    (init, xg_loaded, input_score_ready, score_done, top_ready, picked, xgs_ready, done_ifg, done_o, turned_ifg,
     turned_o, hi_ifg, hi_o, gates_ifg, gates_o, sig_if, tanh_g, sig_o, fc_ready, ig_ready, c_ready, tc_ready,
     h_weight_ready, h_ready, h_hi_ready, h_lo_ready, h_kept) = [sem(n) for n in (
         "init xg_loaded input_score_ready score_done top_ready picked xgs_ready done_ifg done_o turned_ifg "
         "turned_o hi_ifg hi_o gates_ifg gates_o sig_if tanh_g sig_o fc_ready ig_ready c_ready tc_ready "
         "h_weight_ready h_ready h_hi_ready h_lo_ready h_kept").split()]
    w = L.raw[:, 0:BLOCKS, :].bitcast(F16).rearrange("p (s c q) (a k) -> p s c q a k", s=CELLS, c=KC, a=2)
    part_ifg = (0, 12, B.bank[0], done_ifg, turned_ifg, hi_ifg, gates_ifg)
    part_o = (12, 16, B.bank[1], done_o, turned_o, hi_o, gates_o)
    score = B.bank[2][0:1, 0:8]
    idle = B.bank[3]
    with ExitStack() as here:
        xg = sb("xg", [128, CELLS, RING * GC], F32)
        xgs = sb("xgs", [128, GC], F32)
        state = sb("state", [128, 8], F32)
        h_parts = sb("h_parts", [128, KC, 32], F16)
        input_score = sb("input_score", [1, CELLS], F32)
        top = sb("top", [1, 8], F32)
        pick = sb("pick", [1, 8], U32)
        turned = sb("turned", [128, 512], F32)
        hi = sb("hi", [128, GC], F32)
        gates = sb("gates", [128, GC], F32)
        act_out = sb("act_out", [128, GC], F32)
        tc = sb("tc", [128, 4], F32)
        h_weight = sb("h_weight", [128, CELLS, KC], F32)
        fc = sb("fc", [128, 4], F32)
        ig = sb("ig", [128, 4], F32)
        block = here.enter_context(nc.Block())

        @block.sync
        def _(sp):
            for k in range(3):
                sp.dma_start(xg[:, :, k * CHUNK * GC:(k + 1) * CHUNK * GC],
                             B.xg[:, :, k * CHUNK * GC:(k + 1) * CHUNK * GC].rearrange("s p g -> p s g")
                             ).then_inc(xg_loaded, 16)
                sp.wait_ge(xg_loaded, 16 * (k + 1))
            with sp.Fori(3, STEPS // CHUNK) as k:
                sp.wait_ge(init, 1)
                sp.wait_ge(xg_loaded, k * 16)
                sp.wait_ge(xgs_ready, (k - 2) * CHUNK)
                sp.dma_start(xg[:, :, bass.ds((k % 3) * (CHUNK * GC), CHUNK * GC)],
                             B.xg[:, :, bass.ds(k * (CHUNK * GC), CHUNK * GC)].rearrange("s p g -> p s g")
                             ).then_inc(xg_loaded, 16)
            sp.wait_ge(xg_loaded, STEPS // CHUNK * 16)

        @block.gpsimd
        def _(pool):
            def keep(t, n):
                pool.wait_ge(h_ready, n)
                nc.gpsimd.tensor_copy(L.h[:, bass.ds(t * 4, 4)], state[:, 4:8]).then_inc(h_kept, 1)

            keep(0, 1)
            with pool.Fori(1, STEPS) as t:
                keep(t, t + 1)

        @block.scalar
        def _(act):
            def activate(n, ahead=True):
                act.wait_ge(gates_ifg, n)
                nc.scalar.activation(act_out[:, 0:8], gates[:, 0:8], ACT.Sigmoid).then_inc(sig_if, 1)
                nc.scalar.activation(act_out[:, 8:12], gates[:, 8:12], ACT.Tanh).then_inc(tanh_g, 1)
                if ahead:
                    nc.scalar.copy(input_score[:], L.lx[:, bass.ds(n * CELLS, CELLS)]).then_inc(input_score_ready, 1)
                act.wait_ge(gates_o, n)
                nc.scalar.activation(act_out[:, 12:16], gates[:, 12:16], ACT.Sigmoid).then_inc(sig_o, 1)
                act.wait_ge(c_ready, n)
                nc.scalar.activation(tc[:], state[:, 0:4], ACT.Tanh).then_inc(tc_ready, 1)

            activate(1)
            with act.Fori(1, STEPS - 1) as t:
                activate(act.snap(t + 1))
            activate(STEPS, ahead=False)

        @block.tensor
        def _(pe):
            def keep_clock_up(products):
                for _ in range(products):
                    nc.tensor.matmul(idle[:], w[:, 0, 0, 0, 0, 0:128], w[:, 0, 0, 0, 0, :], start=True, stop=True)

            pe.wait_ge(init, 1)
            with pe.Fori(1, STEPS) as t:
                pe.wait_ge(init, 1)
                pe.wait_ge(input_score_ready, t)
                nc.tensor.matmul(score[:, 0:CELLS], B.ones[0:1, 0:1], input_score[:], start=True, stop=False)
                pe.wait_ge(c_ready, t)
                for k in range(KC):
                    nc.tensor.matmul(score[:, 0:CELLS], state[:, k:k + 1], L.wsel[:, :, k], start=False, stop=False)
                pe.wait_ge(h_weight_ready, t)
                pe.wait_ge(tc_ready, t)
                for k in range(KC):
                    last = nc.tensor.matmul(score[:, 0:CELLS], tc[:, k:k + 1], h_weight[:, :, k], start=False,
                                            stop=(k == KC - 1))
                last.then_inc(score_done, 1)
                keep_clock_up(WARM_PICK - 1)
                pe.wait_ge(init, 1)
                pe.wait_ge(h_lo_ready, t)
                keep_clock_up(1)
                pe.wait_ge(init, 1)
                pe.wait_ge(picked, t)
                s = pe.value_load(pick[0:1, 0:1])

                def cell(s):
                    for first, end, bank, done, _, _, _ in (part_ifg, part_o):
                        for c in range(KC):
                            for a in range(2):
                                for q in range(4):
                                    last = nc.tensor.matmul(
                                        bank[32 * q:32 * q + 32, 0:32 * (end - first)], h_parts[:, c, :],
                                        w[:, s, c, q, a, 32 * first:32 * end],
                                        start=(c == 0 and a == 0), stop=(c == KC - 1 and a == 1),
                                        tile_position=(0, 32 * q))
                        last.then_inc(done, 1)

                with pe.If(s < 2):
                    with pe.If(s < 1):
                        cell(0)
                    with pe.Else():
                        cell(1)
                with pe.Else():
                    with pe.If(s < 3):
                        cell(2)
                    with pe.Else():
                        cell(3)
                keep_clock_up(WARM_GATES)

        @block.vector
        def _(dve):
            tv = turned[:].rearrange("p (b m) -> p b m", m=32)

            def turn(part, t):
                first, end, bank, done, turned_part, _, _ = part
                dve.wait_ge(done, t)
                nc.vector.transpose(turned[:, 32 * first:32 * end], bank[:, 0:32 * (end - first)]
                                    ).then_inc(turned_part, 1)

            def add_hi(part, t):
                first, end, _, _, turned_part, hi_part, _ = part
                dve.wait_ge(turned_part, t)
                nc.vector.scalar_tensor_tensor(out=hi[:, first:end], in0=tv[:, first:end, 0], scalar=L.inv[:, 0:1],
                                               in1=xgs[:, first:end], op0=ALU.mult, op1=ALU.add).then_inc(hi_part, 1)

            def add_lo(part, t):
                first, end, _, _, _, hi_part, gates_part = part
                dve.wait_ge(hi_part, t)
                nc.vector.scalar_tensor_tensor(out=gates[:, first:end], in0=tv[:, first:end, 1],
                                               scalar=L.inv[:, 0:1], in1=hi[:, first:end], op0=ALU.mult,
                                               op1=ALU.add).then_inc(gates_part, 1)

            def forget(n):
                dve.wait_ge(sig_if, n)
                nc.vector.tensor_tensor(fc[:], act_out[:, 4:8], state[:, 0:4], ALU.mult).then_inc(fc_ready, 1)

            def new_i(n):
                dve.wait_ge(tanh_g, n)
                nc.vector.tensor_tensor(ig[:], act_out[:, 0:4], act_out[:, 8:12], ALU.mult).then_inc(ig_ready, 1)

            def new_c(n):
                dve.wait_ge(ig_ready, n)
                nc.vector.tensor_tensor(state[:, 0:4], fc[:], ig[:], ALU.add).then_inc(c_ready, 1)

            def weigh_h(n):
                dve.wait_ge(sig_o, n)
                nc.vector.tensor_tensor(h_weight[:], L.wsel[:, :, 4:8], act_out[:, 12:16].rearrange(
                    "p (a k) -> p a k", a=1).to_broadcast((128, CELLS, KC)), ALU.mult).then_inc(h_weight_ready, 1)

            def new_h(n):
                dve.wait_ge(tc_ready, n)
                nc.vector.scalar_tensor_tensor(out=state[:, 4:8], in0=act_out[:, 12:16], scalar=H_SCALE, in1=tc[:],
                                               op0=ALU.mult, op1=ALU.mult).then_inc(h_ready, 1)
                dve.wait_ge(h_ready, n)
                nc.vector.tensor_copy(h_parts[:, :, 0], state[:, 4:8]).then_inc(h_hi_ready, 1)
                dve.wait_ge(h_hi_ready, n)
                nc.vector.tensor_tensor(h_parts[:, :, 1], state[:, 4:8], h_parts[:, :, 0], ALU.subtract
                                        ).then_inc(h_lo_ready, 1)

            def choose(t):
                dve.wait_ge(init, 1)
                dve.wait_ge(score_done, t)
                nc.vector.max(top[:], score).then_inc(top_ready, 1)
                dve.wait_ge(init, 1)
                dve.wait_ge(top_ready, t)
                nc.vector.max_index(pick[:], top[:], score).then_inc(picked, 1)
                dve.wait_ge(init, 1)
                dve.wait_ge(picked, t)
                s = dve.value_load(pick[0:1, 0:1], min_val=0, max_val=CELLS - 1)
                dve.wait_ge(xg_loaded, (t // CHUNK + 1) * 16)
                nc.vector.tensor_copy(xgs[:], xg[:, bass.ds(s, 1), bass.ds((t % RING) * GC, GC)]
                                      ).then_inc(xgs_ready, 1)

            def finish(t, n):
                turn(part_ifg, t)
                dve.wait_ge(xgs_ready, t)
                add_hi(part_ifg, t)
                add_lo(part_ifg, t)
                turn(part_o, t)
                dve.wait_ge(h_kept, t)
                forget(n)
                add_hi(part_o, t)
                new_i(n)
                add_lo(part_o, t)
                new_c(n)
                weigh_h(n)
                new_h(n)

            nc.vector.memset(score, -3e38)
            nc.vector.memset(state[:], 0.0)
            nc.vector.memset(h_parts[:], 0.0).then_inc(init, 1)
            dve.wait_ge(init, 1)
            dve.wait_ge(xg_loaded, 16)
            for first, end, _, _, _, _, gates_part in (part_ifg, part_o):
                nc.vector.tensor_copy(gates[:, first:end], xg[:, 0, first:end]).then_inc(gates_part, 1)
            forget(1)
            new_i(1)
            new_c(1)
            weigh_h(1)
            new_h(1)
            choose(1)
            with dve.Fori(1, STEPS - 1) as t:
                finish(t, t + 1)
                choose(t + 1)
            finish(STEPS - 1, STEPS)


def add_hidden(nc, ctx, B, L):
    turned = nc.alloc_semaphore("hidden_turned")
    h = L.h[:].rearrange("p (t c) -> p t c", c=KC)
    with nc.Block() as block:
        @block.tensor
        def _(pe):
            for m in range(NT):
                for c in range(KC):
                    last = nc.tensor.transpose(B.bank[m][0:R, c * 128:(c + 1) * 128], h[:, m * R:(m + 1) * R, c],
                                               B.ident[:])
                last.then_inc(turned, 1)

        @block.vector
        def _(dve):
            for m in range(NT):
                dve.wait_ge(turned, m + 1)
                for c in range(KC):
                    x = B.x[:, m, :].rearrange("p (q c r) -> p q c r", q=4, c=KC)[:, :, c, :]
                    nc.vector.scalar_tensor_tensor(
                        out=x, in0=B.bank[m][0:R, c * 128:(c + 1) * 128].rearrange("p (q r) -> p q r", q=4),
                        scalar=1.0 / H_SCALE, in1=x, op0=ALU.mult, op1=ALU.add)


HEADS = 4
HID = 256
HH = HEADS * HID


def graph_attention(nc, ctx, B):
    I = B.I
    with ExitStack() as here:
        def sb(name, shape, dt):
            return here.enter_context(nc.sbuf_tensor(name, shape, dt))

        G = Buffers()
        G.absent = sb("gat_absent", [R, NT, N], F32)
        G.h = sb("gat_h", [R, NT, HH], F32)
        G.out = sb("gat_out", [R, NT, HH], F32)
        G.outT = sb("gat_outT", [128, HH // 128, N], F32)
        G.sel = sb("gat_sel", [HEADS, HEADS, R], F32)
        add_self_loops(nc, ctx, B, G)
        xnT = B.xnT[:].rearrange("p (c n) -> p c n", c=KC)
        gat_layer(nc, ctx, B, G, 1, xnT, KC)
        gat_turn(nc, ctx, B, G, 1)
        gat_layer(nc, ctx, B, G, 2, G.outT[:], HH // 128)
        gat_turn(nc, ctx, B, G, 2)
        gat_head(nc, ctx, B, G)


def add_self_loops(nc, ctx, B, G):
    loaded, looped = [nc.alloc_semaphore("loops_" + n) for n in ("loaded", "looped")]
    with nc.Block() as block:
        @block.sync
        def _(sp):
            sp.dma_start(G.sel[:], B.I["c_sel4"].rearrange("h (a r) -> h a r", a=HEADS)).then_inc(loaded, 16)
            sp.wait_ge(loaded, 16)

        @block.vector
        def _(dve):
            for m in range(NT):
                d = B.cnt[:, m, m * R:(m + 1) * R]
                nc.vector.tensor_tensor(d, d, B.ident[0:R, 0:R], ALU.add).then_inc(looped, 1)
            for m in range(NT):
                dve.wait_ge(looped, m + 1)
                nc.vector.tensor_scalar(G.absent[:, m, :], B.cnt[:, m, :], 0.0, -BIG, ALU.is_equal, ALU.mult)


def gat_layer(nc, ctx, B, G, layer, inT, kc):
    I = B.I

    def sb(name, shape, dt):
        return here.enter_context(nc.sbuf_tensor(f"gat{layer}_" + name, shape, dt))

    def sem(name):
        return nc.alloc_semaphore(f"gat{layer}_" + name)

    (w_loaded, v_loaded, h_done, h_kept, step, a_ready, aT_done, aT_ready, row_done, e_ready, leaked, masked, top_ready,
     exp_ready, p_ready, p_turned, pT_kept_a, pT_kept_v, out_done, scaled, kept) = [sem(n) for n in (
         "w_loaded v_loaded h_done h_kept step a_ready aT_done aT_ready row_done e_ready leaked masked top_ready "
         "exp_ready p_ready p_turned pT_kept_a pT_kept_v out_done scaled kept").split()]
    with ExitStack() as here:
        w = sb("w", [128, kc, HH], F32)
        att = sb("att", [R, 2, HH], F32)
        bias = sb("bias", [R, HH], F32)
        prod = sb("prod", [R, 2, HH], F32)
        a = sb("a", [R, 2, NT, HEADS], F32)
        aT = sb("aT", [HEADS, N], F32)
        e = sb("e", [R, 2, N], F32)
        leaky = sb("leaky", [R, 2, N], F32)
        em = sb("em", [R, 2, N], F32)
        top = sb("top", [R, 2], F32)
        neg_top = sb("neg_top", [R, 2], F32)
        p = sb("p", [R, 2, N], F32)
        pT = sb("pT", [R, 2, NT, R], F32)
        total = sb("total", [R, 4], F32)
        inv = sb("inv", [R, 4], F32)
        res = sb("res", [R, 2, HID], F32)
        block = here.enter_context(nc.Block())
        TILES = [(hd, m) for hd in range(HEADS) for m in range(NT)]
        M = len(TILES)

        def row(hd):
            return B.bank[2 * (hd % 2)][0:R, 0:500], B.bank[2 * (hd % 2) + 1][0:R, 0:R]

        @block.sync
        def _(sp):
            sp.dma_start(w[:], I[f"L3_gnn_W{layer}"].rearrange("(c p) n -> p c n", p=128)).then_inc(w_loaded, 16)
            for i, name in enumerate(("src", "dst")):
                sp.dma_start(att[:, i, :], I[f"L3_gnn_att_{name}{layer}"].rearrange("(a h) d -> a (h d)", a=1)
                             .to_broadcast((R, HH))).then_inc(v_loaded, 16)
            sp.dma_start(bias[:], I[f"L3_gnn_b{layer}"].rearrange("(a d) -> a d", a=1).to_broadcast((R, HH))
                         ).then_inc(v_loaded, 16)

        @block.tensor
        def _(pe):
            pe.wait_ge(w_loaded, 16)
            for m in range(NT):
                for half in range(2):
                    i = 2 * m + half
                    if i >= 8:
                        pe.wait_ge(h_kept, i - 7)
                    for c in range(kc):
                        last = nc.tensor.matmul(B.bank[i % 8][0:R, :], inT[:, c, m * R:(m + 1) * R],
                                                w[:, c, half * 512:(half + 1) * 512], start=(c == 0),
                                                stop=(c == kc - 1))
                    last.then_inc(h_done, 1)
            pe.wait_ge(a_ready, 2 * NT)
            pe.wait_ge(h_kept, 2 * NT)
            for m in range(NT):
                o = B.bank[4][0:HEADS, m * R:(m + 1) * R] if m < 4 else B.bank[5][0:HEADS, 0:R]
                last = nc.tensor.transpose(o, a[:, 0, m, :], B.ident[0:R, 0:R])
            last.then_inc(aT_done, 1)
            pe.wait_ge(aT_ready, 2)

            def head_row(hd):
                big, small = row(hd)
                nc.tensor.matmul(big, G.sel[:, hd, :], aT[:, 0:500], start=True, stop=True)
                nc.tensor.matmul(small, G.sel[:, hd, :], aT[:, 500:N], start=True, stop=True).then_inc(row_done, 1)

            def turn(i):
                pe.wait_ge(p_ready, i + 1)
                if i >= 1:
                    pe.wait_ge(pT_kept_a, i)
                    pe.wait_ge(pT_kept_v, i)
                for t in range(NT):
                    o = B.bank[4][0:R, t * R:(t + 1) * R] if t < 4 else B.bank[5][0:R, 0:R]
                    last = nc.tensor.transpose(o, p[:, i % 2, t * R:(t + 1) * R], B.ident[0:R, 0:R])
                last.then_inc(p_turned, 1)

            def gather(i):
                hd, m = TILES[i]
                pe.wait_ge(pT_kept_a, i + 1)
                pe.wait_ge(pT_kept_v, i + 1)
                if i >= 2:
                    pe.wait_ge(scaled, i - 1)
                for t in range(NT):
                    last = nc.tensor.matmul(B.bank[6 + i % 2][0:R, 0:HID], pT[:, i % 2, t, :],
                                            G.h[:, t, hd * HID:(hd + 1) * HID], start=(t == 0),
                                            stop=(t == NT - 1))
                last.then_inc(out_done, 1)

            head_row(0)
            head_row(1)
            turn(0)
            for i, (hd, m) in enumerate(TILES):
                if i + 1 < M:
                    turn(i + 1)
                gather(i)
                if m == NT - 1 and hd + 2 < HEADS:
                    pe.wait_ge(e_ready, NT * (hd + 1))
                    head_row(hd + 2)

        @block.scalar
        def _(act):
            for m in range(NT):
                for half in range(2):
                    i = 2 * m + half
                    act.wait_ge(h_done, i + 1)
                    nc.scalar.copy(G.h[:, m, half * 512:(half + 1) * 512], B.bank[i % 8][0:R, :]).then_inc(h_kept, 1)

            def add_target(i):
                hd, m = TILES[i]
                act.wait_ge(row_done, hd + 1)
                act.wait_ge(a_ready, 2 * NT)
                if i >= 2:
                    act.wait_ge(leaked, i - 1)
                big, small = row(hd)
                nc.scalar.activation(e[:, i % 2, 0:500], big, ACT.Identity, bias=a[:, 1, m, hd:hd + 1])
                nc.scalar.activation(e[:, i % 2, 500:N], small, ACT.Identity, bias=a[:, 1, m, hd:hd + 1]
                                     ).then_inc(e_ready, 1)

            def expo(i):
                act.wait_ge(top_ready, 2 * i + 2)
                if i >= 2:
                    act.wait_ge(p_turned, i - 1)
                nc.scalar.activation(p[:, i % 2, :], em[:, i % 2, :], ACT.Exp, bias=neg_top[:, i % 2:i % 2 + 1]
                                     ).then_inc(exp_ready, 1)

            def keep_turned(i):
                act.wait_ge(p_turned, i + 1)
                if i >= 2:
                    act.wait_ge(out_done, i - 1)
                nc.scalar.copy(pT[:, i % 2, 0:4, :].rearrange("p t r -> p (t r)"), B.bank[4][0:R, 0:500]
                               ).then_inc(pT_kept_a, 1)

            def rectify(i):
                hd, m = TILES[i]
                act.wait_ge(scaled, i + 1)
                nc.scalar.activation(G.out[:, m, hd * HID:(hd + 1) * HID], res[:, i % 2, :], ACT.Relu
                                     ).then_inc(kept, 1)

            add_target(0)
            for i in range(M + 4):
                if i + 1 < M:
                    add_target(i + 1)
                if 1 <= i <= M:
                    expo(i - 1)
                if 2 <= i <= M + 1:
                    keep_turned(i - 2)
                if 4 <= i:
                    rectify(i - 4)

        @block.vector
        def _(dve):
            dve.wait_ge(v_loaded, 48)
            for m in range(NT):
                dve.wait_ge(h_kept, 2 * m + 2)
                for i in range(2):
                    if m > 0:
                        dve.wait_ge(a_ready, 2 * m - 1 + i)
                    nc.vector.tensor_tensor(prod[:, i, :], G.h[:, m, :], att[:, i, :], ALU.mult).then_inc(step, 1)
                    dve.wait_ge(step, 2 * m + i + 1)
                    nc.vector.tensor_reduce(a[:, i, m, :], prod[:, i, :].rearrange("p (h d) -> p h d", h=HEADS),
                                            X_AXIS, ALU.add).then_inc(a_ready, 1)
            dve.wait_ge(aT_done, 1)
            nc.vector.tensor_copy(aT[:, 0:500], B.bank[4][0:HEADS, 0:500]).then_inc(aT_ready, 1)
            nc.vector.tensor_copy(aT[:, 500:N], B.bank[5][0:HEADS, 0:R]).then_inc(aT_ready, 1)

            def leak(i):
                dve.wait_ge(e_ready, i + 1)
                if i >= 2:
                    dve.wait_ge(masked, i - 1)
                nc.vector.scalar_tensor_tensor(out=leaky[:, i % 2, :], in0=e[:, i % 2, :], scalar=0.2,
                                               in1=e[:, i % 2, :], op0=ALU.mult, op1=ALU.max).then_inc(leaked, 1)

            def row_max(i):
                dve.wait_ge(masked, i + 1)
                if i >= 2:
                    dve.wait_ge(exp_ready, i - 1)
                nc.vector.tensor_reduce(top[:, i % 2:i % 2 + 1], em[:, i % 2, :], X_AXIS, ALU.max).then_inc(top_ready, 1)
                dve.wait_ge(top_ready, 2 * i + 1)
                nc.vector.tensor_scalar(neg_top[:, i % 2:i % 2 + 1], top[:, i % 2:i % 2 + 1], -1.0, None, ALU.mult
                                        ).then_inc(top_ready, 1)

            def weigh(i):
                hd, m = TILES[i]
                dve.wait_ge(exp_ready, i + 1)
                nc.vector.tensor_tensor_reduce(p[:, i % 2, :], p[:, i % 2, :], B.cnt[:, m, :], 1.0, 0.0, ALU.mult,
                                               ALU.add, total[:, i % 4:i % 4 + 1]).then_inc(p_ready, 1)

            def keep_turned(i):
                dve.wait_ge(p_turned, i + 1)
                if i >= 2:
                    dve.wait_ge(out_done, i - 1)
                nc.vector.tensor_copy(pT[:, i % 2, 4, :], B.bank[5][0:R, 0:R]).then_inc(pT_kept_v, 1)

            def finish(i):
                hd, m = TILES[i]
                s = slice(i % 4, i % 4 + 1)
                dve.wait_ge(p_ready, i + 1)
                nc.vector.tensor_scalar(total[:, s], total[:, s], 1e-16, None, ALU.add).then_inc(step, 1)
                dve.wait_ge(step, 2 * NT + 2 * i + 1)
                nc.vector.reciprocal(inv[:, s], total[:, s]).then_inc(step, 1)
                dve.wait_ge(step, 2 * NT + 2 * i + 2)
                dve.wait_ge(out_done, i + 1)
                if i >= 2:
                    dve.wait_ge(kept, i - 1)
                nc.vector.scalar_tensor_tensor(out=res[:, i % 2, :], in0=B.bank[6 + i % 2][0:R, 0:HID],
                                               scalar=inv[:, s], in1=bias[:, hd * HID:(hd + 1) * HID],
                                               op0=ALU.mult, op1=ALU.add).then_inc(scaled, 1)

            leak(0)
            for i in range(M + 3):
                if i + 1 < M:
                    leak(i + 1)
                if i < M:
                    row_max(i)
                if 1 <= i <= M:
                    weigh(i - 1)
                if 2 <= i <= M + 1:
                    keep_turned(i - 2)
                if i >= 3:
                    finish(i - 3)

        @block.gpsimd
        def _(pool):
            for i, (hd, m) in enumerate(TILES):
                pool.wait_ge(leaked, i + 1)
                if i >= 2:
                    pool.wait_ge(exp_ready, i - 1)
                nc.gpsimd.tensor_tensor(em[:, i % 2, :], leaky[:, i % 2, :], G.absent[:, m, :], ALU.add
                                        ).then_inc(masked, 1)


def gat_turn(nc, ctx, B, G, layer):
    turned, kept_a, kept_v = [nc.alloc_semaphore(f"gat_turn{layer}_{n}")
                              for n in ("turned", "kept_a", "kept_v")]
    C = HH // 128
    with nc.Block() as block:
        @block.tensor
        def _(pe):
            for c in range(C):
                if c >= 4:
                    pe.wait_ge(kept_a, c - 3)
                    pe.wait_ge(kept_v, c - 3)
                for m in range(NT):
                    b = 2 * (c % 4)
                    o = B.bank[b][:, m * R:(m + 1) * R] if m < 4 else B.bank[b + 1][:, 0:R]
                    last = nc.tensor.transpose(o, G.out[:, m, c * 128:(c + 1) * 128], B.ident[0:R, 0:R])
                last.then_inc(turned, 1)

        @block.scalar
        def _(act):
            for c in range(C):
                act.wait_ge(turned, c + 1)
                nc.scalar.copy(G.outT[:, c, 0:500], B.bank[2 * (c % 4)][:, 0:500]).then_inc(kept_a, 1)

        @block.vector
        def _(dve):
            for c in range(C):
                dve.wait_ge(turned, c + 1)
                nc.vector.tensor_copy(G.outT[:, c, 500:N], B.bank[2 * (c % 4) + 1][:, 0:R]).then_inc(kept_v, 1)


def gat_head(nc, ctx, B, G):
    I = B.I
    loaded, done = [nc.alloc_semaphore("fc_" + n) for n in ("loaded", "done")]
    C = HH // 128
    with ExitStack() as here:
        w = here.enter_context(nc.sbuf_tensor("fc_w", [128, C, D], F32))
        bias = here.enter_context(nc.sbuf_tensor("fc_bias", [1, D], F32))
        block = here.enter_context(nc.Block())

        @block.sync
        def _(sp):
            sp.dma_start(w[:], I["L3_gnn_fcW"].rearrange("(c p) n -> p c n", p=128)).then_inc(loaded, 16)
            sp.dma_start(bias[:], I["L3_gnn_fcb"].rearrange("(a d) -> a d", a=1)).then_inc(loaded, 16)

        @block.tensor
        def _(pe):
            pe.wait_ge(loaded, 32)
            for m in range(NT):
                nc.tensor.matmul(B.bank[m][0:R, :], B.ones[0:1, 0:R], bias[:], start=True, stop=False)
                for c in range(C):
                    last = nc.tensor.matmul(B.bank[m][0:R, :], G.outT[:, c, m * R:(m + 1) * R], w[:, c, :],
                                            start=False, stop=(c == C - 1))
                last.then_inc(done, 1)

        @block.vector
        def _(dve):
            for m in range(NT):
                dve.wait_ge(done, m + 1)
                nc.vector.tensor_tensor(B.x[:, m, :], B.x[:, m, :], B.bank[m][0:R, :], ALU.add)


AH = 8
DK = D // AH
KV = (8, 4, 1)


def routed_attention(nc, ctx, B):
    I = B.I
    NK = len(KV)

    def sb(name, shape, dt):
        return here.enter_context(nc.sbuf_tensor("att_" + name, shape, dt))

    def sem(name):
        return nc.alloc_semaphore("att_" + name)

    (r_loaded, mean_step, hidden_done, hidden_ready, logit_done, pick_step, exp_done, hot_ready, hot_wide,
     hot_kept, w_mixed, added, qk_done, qk_kept, v_done, v_kept, s_done, max_step, max_ready, exp_ready, inv_step,
     inv_ready, p_ready, p_turned, pT_kept_a, pT_kept_v, o_done, o_kept, out_done) = [sem(n) for n in (
         "r_loaded mean_step hidden_done hidden_ready logit_done pick_step exp_done hot_ready hot_wide "
         "hot_kept w_mixed added qk_done qk_kept v_done v_kept s_done max_step max_ready exp_ready inv_step "
         "inv_ready p_ready p_turned pT_kept_a pT_kept_v o_done o_kept out_done").split()]
    STAGES = 3
    w_loaded = [sem(f"w_loaded{i}") for i in range(STAGES)]
    xnT = B.xnT[:].rearrange("p (c n) -> p c n", c=KC)
    PAIRS = [(w, i) for w in "qkvo" for i in range(NK)]
    TILES = [(hd, m) for hd in range(AH) for m in range(NT)]
    M = len(TILES)
    with ExitStack() as here:
        r1 = sb("r1", [128, KC, 128], F32)
        rb1 = sb("rb1", [128, 1], F32)
        r2 = sb("r2", [128, NK], F32)
        rb2 = sb("rb2", [1, NK], F32)
        total = sb("total", [128, KC], F32)
        mean = sb("mean", [128, KC], F32)
        hidden = sb("hidden", [128, 1], F32)
        logit = sb("logit", [1, 8], F32)
        top = sb("top", [1, 8], F32)
        neg_top = sb("neg_top", [1, 1], F32)
        score = sb("score", [1, 8], F32)
        best = sb("best", [1, 8], F32)
        pick = sb("pick", [1, 8], U32)
        pickf = sb("pickf", [1, 1], F32)
        hot = sb("hot", [1, NK], F32)
        hots = sb("hots", [128, NK], F32)
        wstage = sb("wstage", [128, STAGES, KC, D], F32)
        wmix = sb("wmix", [128, 4, KC, D], F32)
        qT = sb("qT", [128, KC, N], F32)
        kT = sb("kT", [128, KC, N], F32)
        v = sb("v", [R, NT, D], F32)
        mx = sb("mx", [R, 2, 2], F32)
        nmx = sb("nmx", [R, 2], F32)
        p = sb("p", [R, 2, N], F32)
        s2 = sb("s2", [R, 2, 2], F32)
        ssum = sb("ssum", [R, 2], F32)
        inv = sb("inv", [R, 2], F32)
        pT = sb("pT", [R, 2, NT, N], F32)
        oT = sb("oT", [128, KC, N], F32)
        block = here.enter_context(nc.Block())

        @block.sync
        def _(sp):
            sp.dma_start(r1[:], I["L3_ffn_r_w1"].rearrange("(c p) n -> p c n", p=128)).then_inc(r_loaded, 16)
            sp.dma_start(rb1[:], I["L3_ffn_r_b1"].rearrange("(p a) -> p a", a=1)).then_inc(r_loaded, 16)
            sp.dma_start(r2[:], I["L3_ffn_r_w2"]).then_inc(r_loaded, 16)
            sp.dma_start(rb2[:], I["L3_ffn_r_b2"].rearrange("(a d) -> a d", a=1)).then_inc(r_loaded, 16)
            for n, (w, i) in enumerate(PAIRS):
                width = KV[i] * DK if w in "kv" else D
                if n >= STAGES:
                    sp.wait_ge(w_mixed, n - STAGES + 1)
                sp.dma_start(wstage[:, n % STAGES, :, 0:width],
                             I[f"L3_ffn_w{w}{i}"].rearrange("(c p) n -> p c n", p=128)
                             ).then_inc(w_loaded[n % STAGES], 16)

        @block.vector
        def _(dve):
            nc.vector.memset(logit[:], -BIG).then_inc(mean_step, 1)
            nc.vector.tensor_reduce(total[:], xnT, X_AXIS, ALU.add).then_inc(mean_step, 1)
            dve.wait_ge(mean_step, 2)
            nc.vector.tensor_scalar(mean[:], total[:], 1.0 / N, None, ALU.mult).then_inc(mean_step, 1)
            dve.wait_ge(logit_done, 1)
            nc.vector.tensor_copy(logit[:, 0:NK], B.bank[1][0:1, 0:NK]).then_inc(pick_step, 1)
            dve.wait_ge(pick_step, 1)
            nc.vector.max(top[:], logit[:]).then_inc(pick_step, 1)
            dve.wait_ge(pick_step, 2)
            nc.vector.tensor_scalar(neg_top[:], top[:, 0:1], -1.0, None, ALU.mult).then_inc(pick_step, 1)
            dve.wait_ge(exp_done, 1)
            nc.vector.max(best[:], score[:]).then_inc(pick_step, 1)
            dve.wait_ge(pick_step, 4)
            nc.vector.max_index(pick[:], best[:], score[:]).then_inc(pick_step, 1)
            dve.wait_ge(pick_step, 5)
            nc.vector.tensor_copy(pickf[:], pick[:, 0:1]).then_inc(pick_step, 1)
            dve.wait_ge(pick_step, 6)
            nc.vector.tensor_scalar(hot[:], B.iota_f[0:1, 0:NK], pickf[:], None, ALU.is_equal).then_inc(hot_ready, 1)
            dve.wait_ge(hot_wide, 1)
            nc.vector.tensor_copy(hots[:], B.bank[2][:, 0:NK]).then_inc(hot_kept, 1)
            dve.wait_ge(hot_kept, 1)
            for n, (w, i) in enumerate(PAIRS):
                dve.wait_ge(w_loaded[n % STAGES], 16 * (n // STAGES + 1))
                kv = KV[i] if w in "kv" else AH
                if i > 0:
                    dve.wait_ge(w_mixed, n)
                rep = AH // kv
                for c in range(KC):
                    whole = wmix[:, n // NK, c, :].rearrange("p (g r d) -> p g r d", g=kv, r=rep)
                    heads = wstage[:, n % STAGES, c, 0:kv * DK].rearrange("p (g d) -> p g d", g=kv)
                    for r in range(rep):
                        out = whole[:, :, r, :]
                        if i == 0:
                            last = nc.vector.tensor_scalar(out, heads, hots[:, 0:1], None, ALU.mult)
                        else:
                            last = nc.vector.scalar_tensor_tensor(out=out, in0=heads, scalar=hots[:, i:i + 1],
                                                                  in1=out, op0=ALU.mult, op1=ALU.add)
                last.then_inc(w_mixed, 1)
            for n in range(2 * KC):
                dve.wait_ge(qk_done, n + 1)
                dst = (qT, kT)[n // KC]
                b = 2 * (n % 2)
                nc.vector.tensor_copy(dst[:, n % KC, 500:N], B.bank[b + 1][:, 0:R]).then_inc(v_kept, 1)
            for m in range(NT):
                dve.wait_ge(v_done, m + 1)
                nc.vector.tensor_copy(v[:, m, :], B.bank[4 + m % 4][0:R, :]).then_inc(v_kept, 1)

            def row_max(i):
                b, s = 2 * (i % 2), slice(i % 2, i % 2 + 1)
                dve.wait_ge(s_done, i + 1)
                nc.vector.tensor_reduce(mx[:, i % 2, 0:1], B.bank[b][0:R, 0:500], X_AXIS, ALU.max).then_inc(max_step, 1)
                nc.vector.tensor_reduce(mx[:, i % 2, 1:2], B.bank[b + 1][0:R, 0:R], X_AXIS, ALU.max
                                        ).then_inc(max_step, 1)
                dve.wait_ge(max_step, 2 * i + 2)
                nc.vector.tensor_scalar(nmx[:, s], mx[:, i % 2, 0:1], mx[:, i % 2, 1:2], -(DK ** -0.5), ALU.max,
                                        ALU.mult).then_inc(max_ready, 1)

            def normalize(i):
                s = slice(i % 2, i % 2 + 1)
                dve.wait_ge(exp_ready, i + 1)
                nc.vector.tensor_tensor(ssum[:, s], s2[:, i % 2, 0:1], s2[:, i % 2, 1:2], ALU.add).then_inc(inv_step, 1)
                dve.wait_ge(inv_step, 2 * i + 1)
                nc.vector.reciprocal(inv[:, s], ssum[:, s]).then_inc(inv_step, 1)
                dve.wait_ge(inv_step, 2 * i + 2)
                nc.vector.tensor_scalar(p[:, i % 2, :], p[:, i % 2, :], inv[:, s], None, ALU.mult).then_inc(p_ready, 1)

            def keep_turned(i):
                hd, m = TILES[i]
                dve.wait_ge(p_turned, i + 1)
                if hd >= 2:
                    dve.wait_ge(o_done, hd - 1)
                nc.vector.tensor_copy(pT[:, hd % 2, 4, m * R:(m + 1) * R], B.bank[5][0:R, 0:R]).then_inc(pT_kept_v, 1)

            def keep_out(hd):
                dve.wait_ge(o_done, hd + 1)
                lo = DK * (hd % 2)
                nc.vector.tensor_copy(oT[lo:lo + DK, hd // 2, 500:N], B.bank[7][lo:lo + DK, 0:R]).then_inc(o_kept, 1)

            for i in range(M + 2):
                if i >= 2:
                    keep_turned(i - 2)
                    if (i - 2) % NT == 1 and i - 2 > NT:
                        keep_out((i - 2) // NT - 1)
                if 1 <= i <= M:
                    normalize(i - 1)
                if i < M:
                    row_max(i)
            keep_out(AH - 1)
            for m in range(NT):
                dve.wait_ge(out_done, m + 1)
                nc.vector.tensor_tensor(B.x[:, m, :], B.x[:, m, :], B.bank[m % 4][0:R, :], ALU.add
                                        ).then_inc(added, 1)

        @block.scalar
        def _(act):
            act.wait_ge(hidden_done, 1)
            nc.scalar.activation(hidden[:], B.bank[0][:, 0:1], ACT.Relu, bias=rb1[:]).then_inc(hidden_ready, 1)
            act.wait_ge(pick_step, 3)
            nc.scalar.activation(score[:], logit[:], ACT.Exp, bias=neg_top[:]).then_inc(exp_done, 1)
            for n in range(2 * KC):
                act.wait_ge(qk_done, n + 1)
                dst = (qT, kT)[n // KC]
                nc.scalar.copy(dst[:, n % KC, 0:500], B.bank[2 * (n % 2)][:, 0:500]).then_inc(qk_kept, 1)

            def expo(i):
                b = 2 * (i % 2)
                act.wait_ge(max_ready, i + 1)
                if i >= 2:
                    act.wait_ge(p_turned, i - 1)
                    act.wait_ge(inv_step, 2 * (i - 2) + 1)
                nc.scalar.activation(p[:, i % 2, 0:500], B.bank[b][0:R, 0:500], ACT.Exp, bias=nmx[:, i % 2:i % 2 + 1],
                                     scale=DK ** -0.5, accum_out=s2[:, i % 2, 0:1])
                nc.scalar.activation(p[:, i % 2, 500:N], B.bank[b + 1][0:R, 0:R], ACT.Exp,
                                     bias=nmx[:, i % 2:i % 2 + 1], scale=DK ** -0.5, accum_out=s2[:, i % 2, 1:2]
                                     ).then_inc(exp_ready, 1)

            def keep_turned(i):
                hd, m = TILES[i]
                act.wait_ge(p_turned, i + 1)
                if hd >= 2:
                    act.wait_ge(o_done, hd - 1)
                nc.scalar.copy(pT[:, hd % 2, 0:4, m * R:(m + 1) * R],
                               B.bank[4][0:R, 0:500].rearrange("p (t r) -> p t r", t=4)).then_inc(pT_kept_a, 1)

            def keep_out(hd):
                act.wait_ge(o_done, hd + 1)
                lo = DK * (hd % 2)
                nc.scalar.copy(oT[lo:lo + DK, hd // 2, 0:500], B.bank[6][lo:lo + DK, 0:500]).then_inc(o_kept, 1)

            for i in range(M + 2):
                if i >= 2:
                    keep_turned(i - 2)
                    if (i - 2) % NT == 1 and i - 2 > NT:
                        keep_out((i - 2) // NT - 1)
                if i < M:
                    expo(i)
            keep_out(AH - 1)

        @block.tensor
        def _(pe):
            pe.wait_ge(r_loaded, 64)
            pe.wait_ge(mean_step, 3)
            for c in range(KC):
                last = nc.tensor.matmul(B.bank[0][:, 0:1], r1[:, c, :], mean[:, c:c + 1], start=(c == 0),
                                        stop=(c == KC - 1))
            last.then_inc(hidden_done, 1)
            pe.wait_ge(hidden_ready, 1)
            nc.tensor.matmul(B.bank[1][0:1, 0:NK], B.ones[0:1, 0:1], rb2[:], start=True, stop=False)
            nc.tensor.matmul(B.bank[1][0:1, 0:NK], hidden[:], r2[:], start=False, stop=True).then_inc(logit_done, 1)
            pe.wait_ge(hot_ready, 1)
            nc.tensor.matmul(B.bank[2][:, 0:NK], B.ones[0:1, :], hot[:], start=True, stop=True).then_inc(hot_wide, 1)
            pe.wait_ge(hot_kept, 1)
            for n in range(2 * KC):
                which, c2 = n // KC, n % KC
                pe.wait_ge(w_mixed, NK * (which + 1))
                if n >= 2:
                    pe.wait_ge(qk_kept, n - 1)
                    pe.wait_ge(v_kept, n - 1)
                b = 2 * (n % 2)
                for c in range(KC):
                    wt = wmix[:, which, c, c2 * 128:(c2 + 1) * 128]
                    nc.tensor.matmul(B.bank[b][:, 0:500], wt, xnT[:, c, 0:500], start=(c == 0), stop=(c == KC - 1))
                    last = nc.tensor.matmul(B.bank[b + 1][:, 0:R], wt, xnT[:, c, 500:N], start=(c == 0),
                                            stop=(c == KC - 1))
                last.then_inc(qk_done, 1)
            pe.wait_ge(w_mixed, 3 * NK)
            for m in range(NT):
                if m >= 4:
                    pe.wait_ge(v_kept, 2 * KC + m - 3)
                for c in range(KC):
                    last = nc.tensor.matmul(B.bank[4 + m % 4][0:R, :], xnT[:, c, m * R:(m + 1) * R], wmix[:, 2, c, :],
                                            start=(c == 0), stop=(c == KC - 1))
                last.then_inc(v_done, 1)
            pe.wait_ge(qk_kept, 2 * KC)
            pe.wait_ge(v_kept, 2 * KC + NT)

            def scores(i):
                hd, m = TILES[i]
                lo, b = DK * (hd % 2), 2 * (i % 2)
                if i >= 2:
                    pe.wait_ge(exp_ready, i - 1)
                q = qT[lo:lo + DK, hd // 2, m * R:(m + 1) * R]
                nc.tensor.matmul(B.bank[b][0:R, 0:500], q, kT[lo:lo + DK, hd // 2, 0:500], start=True, stop=True)
                nc.tensor.matmul(B.bank[b + 1][0:R, 0:R], q, kT[lo:lo + DK, hd // 2, 500:N], start=True, stop=True
                                 ).then_inc(s_done, 1)

            def turn(i):
                pe.wait_ge(p_ready, i + 1)
                if i >= 1:
                    pe.wait_ge(pT_kept_a, i)
                    pe.wait_ge(pT_kept_v, i)
                for t in range(NT):
                    o = B.bank[4][0:R, t * R:(t + 1) * R] if t < 4 else B.bank[5][0:R, 0:R]
                    last = nc.tensor.transpose(o, p[:, i % 2, t * R:(t + 1) * R], B.ident[0:R, 0:R])
                last.then_inc(p_turned, 1)

            def sum_head(hd):
                lo = DK * (hd % 2)
                pe.wait_ge(pT_kept_a, NT * (hd + 1))
                pe.wait_ge(pT_kept_v, NT * (hd + 1))
                if hd >= 1:
                    pe.wait_ge(o_kept, 2 * hd)
                for t in range(NT):
                    vt = v[:, t, hd * DK:(hd + 1) * DK]
                    nc.tensor.matmul(B.bank[6][lo:lo + DK, 0:500], vt, pT[:, hd % 2, t, 0:500], start=(t == 0),
                                     stop=(t == NT - 1))
                    last = nc.tensor.matmul(B.bank[7][lo:lo + DK, 0:R], vt, pT[:, hd % 2, t, 500:N],
                                            start=(t == 0), stop=(t == NT - 1))
                last.then_inc(o_done, 1)

            scores(0)
            scores(1)
            for i in range(M):
                turn(i)
                if i + 2 < M:
                    scores(i + 2)
                if i % NT == 0 and i > 0:
                    sum_head(i // NT - 1)
            sum_head(AH - 1)
            pe.wait_ge(o_kept, 2 * AH)
            pe.wait_ge(w_mixed, 4 * NK)
            for m in range(NT):
                if m >= 4:
                    pe.wait_ge(added, m - 3)
                for c in range(KC):
                    last = nc.tensor.matmul(B.bank[m % 4][0:R, :], oT[:, c, m * R:(m + 1) * R], wmix[:, 3, c, :],
                                            start=(c == 0), stop=(c == KC - 1))
                last.then_inc(out_done, 1)


def store(nc, ctx, B, out):
    stored = nc.alloc_semaphore("out_stored")
    with nc.Block() as block:
        @block.sync
        def _(sp):
            sp.dma_start(out.rearrange("(j p) d -> p j d", p=R), B.x[:]).then_inc(stored, 16)
            sp.wait_ge(stored, 16)


def program(nc, I, out):
    with ExitStack() as ctx:
        B = allocate(nc, ctx, I)
        load_constants(nc, B)
        for stage in (count_edges, chebyshev, route_expert, gcn, choose_experts, relational, lstm, graph_attention,
                      routed_attention):
            if stage is not count_edges:
                layernorm(nc, B)
            with nc.cleanup_on_exit():
                stage(nc, ctx, B)
        store(nc, ctx, B, out)


def lay_out(inputs):
    import numpy as np
    out = {k: np.ascontiguousarray(v) for k, v in inputs.items()}
    out["c_ident"] = np.eye(128, dtype=np.float32)
    out["c_w_compT"] = np.ascontiguousarray(out.pop("L2_gnn_w_comp").T)
    out["c_same16"] = np.tile(np.eye(16, dtype=np.float32), (8, 1))
    out["c_sel4"] = np.kron(np.eye(4, dtype=np.float32), np.ones((1, 125), np.float32))
    w = out.pop("L2_ffn_W_ih").reshape(4, 4, 4, 4, 32, 4, 128)
    w = w.transpose(0, 6, 5, 1, 3, 2, 4).reshape(4, 128, 4, 2, 8, 128)
    out["c_w_ih"] = np.ascontiguousarray(w)
    w = out.pop("L2_ffn_W_hh").reshape(4, 4, 4, 4, 32, 4, 4, 32)
    out["c_w_hh"] = np.ascontiguousarray(w.transpose(0, 5, 7, 6, 2, 1, 3, 4).reshape(4, 128, 16, 512))
    for name in ("b_ih", "b_hh"):
        b = out.pop("L2_ffn_" + name).reshape(4, 4, 4, 4, 32)
        out["c_" + name] = np.ascontiguousarray(b.transpose(2, 4, 0, 1, 3).reshape(128, 64))
    w = out.pop("L2_ffn_W_sel")
    h, c = (w[:, i * 512:(i + 1) * 512].reshape(4, 4, 4, 32).transpose(1, 3, 0, 2).reshape(128, 4, 4)
            for i in range(2))
    out["c_w_sel_state"] = np.ascontiguousarray(np.concatenate([c, h], 2))
    out["c_w_sel_x"] = np.ascontiguousarray(w[:, 1024:].reshape(4, 4, 128).transpose(2, 1, 0))
    return out




def kernel(**inputs):
    import numpy as _np
    import concourse.bacc as _bacc
    from concourse import mybir as _mybir
    from concourse.bass_utils import run_bass_kernel_spmd as _run

    nc = _bacc.Bacc("TRN2", target_bir_lowering=False, num_devices=1)
    arrays, aps = {}, {}
    for name, a in lay_out(inputs).items():
        arrays[f"in_{name}"] = a
        aps[name] = nc.dram_tensor(f"in_{name}", a.shape, _mybir.dt.from_np(a.dtype), kind="ExternalInput").ap()
    out = nc.dram_tensor("out_0", (625, 512), _mybir.dt.from_np(_np.dtype("float32")), kind="ExternalOutput").ap()
    program(nc, aps, out)
    r = _run(nc, [arrays], core_ids=[0])
    return r.results[0]["out_0"]
```
